# Optimizing a Trainium2 kernel written in Bass

```python
import numpy as np
import jax
import jax.numpy as jnp

def _softmax(x, axis=-1):
    return jax.nn.softmax(x, axis=axis)

def _gelu(x):
    return jax.nn.gelu(x, approximate=True)

def _silu(x):
    return jax.nn.silu(x)

def _sigmoid(x):
    return jax.nn.sigmoid(x)

def _layernorm(x, axis=-1, eps=1e-05):
    m = jnp.mean(x, axis=axis, keepdims=True)
    v = jnp.var(x, axis=axis, keepdims=True)
    return (x - m) / jnp.sqrt(v + eps)

def _scatter_add(tgt, idx, src, axis=0):
    return tgt.at[idx].add(src)

def _segment_sum(src, seg, n):
    return jax.ops.segment_sum(src, seg, n)
kernel_name = 'mk_decoder_postln_d1_seqx_r4_fdb982'

def setup_inputs(seed: int=0):
    np.random.seed(seed)
    _w = jnp.asarray

    def _rec_inputs():
        import jax
        import jax.numpy as jnp
        _rk = jax.random.key(seed)
        x = -0.0002928 + 1 * jax.random.normal(jax.random.fold_in(_rk, 1), (8, 512, 256), jnp.float32)
        _lenS = 512 - jax.random.randint(jax.random.fold_in(_rk, 7), (8,), 0, max(1, 512 // 4) + 1, jnp.int32)
        _lenS2 = 512 - jax.random.randint(jax.random.fold_in(_rk, 8), (8,), 0, max(1, 512 // 4) + 1, jnp.int32)
        _ctx_1024P = jax.random.normal(jax.random.fold_in(_rk, 11), (8, 16, 256), jnp.float32)
        _ctx_1024c = jax.random.dirichlet(jax.random.fold_in(_rk, 511), 0.3 * jnp.ones((16,), jnp.float32), (8, 512))
        _ctx_1024t = jnp.einsum('bsk,bkd->bsd', _ctx_1024c, _ctx_1024P)
        _ctx_1024t = _ctx_1024t * jax.lax.rsqrt(jnp.mean(jnp.square(_ctx_1024t)) + 1e-12) * 0.953939
        ctx_1024 = -1.39393e-06 + 0.999914 * (_ctx_1024t + 0.3 * jax.random.normal(jax.random.fold_in(_rk, 611), (8, 512, 256), jnp.float32))
        return (x, ctx_1024)
    x, ctx_1024 = _rec_inputs()

    def _L0_attn_setup():
        import jax, jax.numpy as jnp
        import numpy as np
        N_HEADS = 16

        def _rotate_half(t):
            shp = t.shape
            t2 = t.reshape(*shp[:-1], shp[-1] // 2, 2)
            return jnp.stack((-t2[..., 1], t2[..., 0]), axis=-1).reshape(shp)
        key = jax.random.key(seed)
        k1, k2, k3 = jax.random.split(key, 3)
        B, N, D = (2, 512, 256)
        x = jax.random.normal(k1, (B, N, D), dtype=jnp.float32)
        w_qkv = jax.random.normal(k2, (D, 3 * D), dtype=jnp.float32) * D ** (-0.5)
        w_proj = jax.random.normal(k3, (D, D), dtype=jnp.float32) * D ** (-0.5)
        return {'x': x, 'w_qkv': w_qkv, 'w_proj': w_proj}
    _L0_attn_all = _L0_attn_setup()
    _L0_attn_in = {k: v for k, v in _L0_attn_all.items() if k in ('w_qkv', 'w_proj')}
    del _L0_attn_all

    def _L0_xattn_setup():
        import jax, jax.numpy as jnp
        import numpy as np
        D_MODEL = 256
        NUM_HEADS = 16
        D_K = D_MODEL // NUM_HEADS
        key = jax.random.key(seed)
        ks = jax.random.split(key, 11)
        B, S, D = (2, 512, D_MODEL)
        scale = 1.0 / np.sqrt(D)
        inp = {'q': jax.random.normal(ks[0], (B, S, D), jnp.float32), 'k': jax.random.normal(ks[1], (B, S, D), jnp.float32), 'v': jax.random.normal(ks[2], (B, S, D), jnp.float32), 'Wq': jax.random.normal(ks[3], (D, D), jnp.float32) * scale, 'bq': jax.random.normal(ks[4], (D,), jnp.float32) * scale, 'Wk': jax.random.normal(ks[5], (D, D), jnp.float32) * scale, 'bk': jax.random.normal(ks[6], (D,), jnp.float32) * scale, 'Wv': jax.random.normal(ks[7], (D, D), jnp.float32) * scale, 'bv': jax.random.normal(ks[8], (D,), jnp.float32) * scale, 'Wo': jax.random.normal(ks[9], (D, D), jnp.float32) * scale, 'bo': jax.random.normal(ks[10], (D,), jnp.float32) * scale}
        return inp
    _L0_xattn_all = _L0_xattn_setup()
    _L0_xattn_in = {k: v for k, v in _L0_xattn_all.items() if k in ('Wq', 'bq', 'Wk', 'bk', 'Wv', 'bv', 'Wo', 'bo')}
    del _L0_xattn_all

    def _L0_ffn_setup():
        import jax, jax.numpy as jnp
        import numpy as np
        DIM = 256
        DEPTH = 2
        HEADS = 8
        DIM_HEAD = 64
        WINDOW = 128
        INNER = HEADS * DIM_HEAD
        HID = int(DIM * 4 * 2 / 3)
        B, N = (2, 2048)
        QK_SCALE = 8.0

        def shift_token(t):
            t1, t2 = jnp.split(t, 2, axis=-1)
            t2 = jnp.pad(t2, ((0, 0), (1, 0), (0, 0)))[:, :-1]
            return jnp.concatenate([t1, t2], axis=-1)

        def l2norm(t):
            return t / jnp.clip(jnp.linalg.norm(t, axis=-1, keepdims=True), 1e-12)

        def rotate_half(x):
            x1, x2 = jnp.split(x, 2, axis=-1)
            return jnp.concatenate([-x2, x1], axis=-1)

        def rotary_xpos(q, k):
            n = q.shape[-2]
            half_idx = jnp.arange(0, DIM_HEAD, 2, dtype=jnp.float32)
            inv_freq = 1.0 / 10000.0 ** (half_idx / DIM_HEAD)
            t = jnp.arange(n, dtype=jnp.float32)
            freqs = t[:, None] * inv_freq[None, :]
            freqs = jnp.concatenate([freqs, freqs], axis=-1)
            base = (half_idx + 0.4 * DIM_HEAD) / (1.4 * DIM_HEAD)
            power = (t - n // 2) / float(WINDOW // 2)
            scale = base[None, :] ** power[:, None]
            scale = jnp.concatenate([scale, scale], axis=-1)
            cos, sin = (jnp.cos(freqs), jnp.sin(freqs))
            q = q * cos * scale + rotate_half(q) * sin * scale
            k = k * cos / scale + rotate_half(k) * sin / scale
            return (q, k)

        def local_attention(q, k, v):
            b, h, n, d = q.shape
            w = n // WINDOW
            bq = q.reshape(b, h, w, WINDOW, d) * QK_SCALE
            bk = k.reshape(b, h, w, WINDOW, d)
            bv = v.reshape(b, h, w, WINDOW, d)

            def look_around(t):
                p = jnp.pad(t, ((0, 0), (0, 0), (1, 0), (0, 0), (0, 0)))
                return jnp.concatenate([p[:, :, :w], p[:, :, 1:]], axis=3)
            bk, bv = (look_around(bk), look_around(bv))
            bt = jnp.arange(n).reshape(w, WINDOW)
            btp = jnp.pad(bt, ((1, 0), (0, 0)), constant_values=-1)
            btk = jnp.concatenate([btp[:w], btp[1:]], axis=1)
            sim = jnp.einsum('bhwid,bhwjd->bhwij', bq, bk)
            i = bt[:, :, None]
            j = btk[:, None, :]
            mask = (i < j) | (i > j + WINDOW) | (j == -1)
            sim = jnp.where(mask, -jnp.finfo(sim.dtype).max, sim)
            attn = jax.nn.softmax(sim, axis=-1)
            out = jnp.einsum('bhwij,bhwjd->bhwid', attn, bv)
            return out.reshape(b, h, n, d)

        def _layer(x, wqkv, qs, ksc, wo, lg, lb, w1, b1, w2, b2):
            b, n, _ = x.shape
            h = shift_token(x)
            qkv = h @ wqkv
            q, k, v = jnp.split(qkv, 3, axis=-1)
            to_heads = lambda t: t.reshape(b, n, HEADS, DIM_HEAD).transpose(0, 2, 1, 3)
            q, k, v = (to_heads(q), to_heads(k), to_heads(v))
            q = l2norm(q) * qs
            k = l2norm(k) * ksc
            q, k = rotary_xpos(q, k)
            o = local_attention(q, k, v)
            o = o.transpose(0, 2, 1, 3).reshape(b, n, INNER)
            x = x + o @ wo
            h = shift_token(x)
            mu = h.mean(-1, keepdims=True)
            var = h.var(-1, keepdims=True)
            h = (h - mu) / jnp.sqrt(var + 1e-05) * lg + lb
            h = h @ w1 + b1
            a, g = jnp.split(h, 2, axis=-1)
            h = a * jax.nn.gelu(g, approximate=False)
            x = x + h @ w2 + b2
            return x
        key = jax.random.key(seed)
        ks = jax.random.split(key, 6)
        return {'x': jax.random.normal(ks[0], (B, N, DIM), jnp.float32), 'wqkv': jax.random.normal(ks[1], (DEPTH, DIM, 3 * INNER), jnp.float32) * 0.02, 'q_scale': jnp.ones((DEPTH, DIM_HEAD), jnp.float32), 'k_scale': jnp.ones((DEPTH, DIM_HEAD), jnp.float32), 'wo': jax.random.normal(ks[2], (DEPTH, INNER, DIM), jnp.float32) * 0.02, 'ln_g': jnp.ones((DEPTH, DIM), jnp.float32), 'ln_b': jnp.zeros((DEPTH, DIM), jnp.float32), 'w1': jax.random.normal(ks[3], (DEPTH, DIM, 2 * HID), jnp.float32) * 0.02, 'b1': jnp.zeros((DEPTH, 2 * HID), jnp.float32), 'w2': jax.random.normal(ks[4], (DEPTH, HID, DIM), jnp.float32) * 0.02, 'b2': jnp.zeros((DEPTH, DIM), jnp.float32)}
    _L0_ffn_all = _L0_ffn_setup()
    _L0_ffn_in = {k: v for k, v in _L0_ffn_all.items() if k in ('wqkv', 'q_scale', 'k_scale', 'wo', 'ln_g', 'ln_b', 'w1', 'b1', 'w2', 'b2')}
    del _L0_ffn_all
    return {'x': x, 'ctx_1024': ctx_1024, 'L0_attn_w_qkv': _L0_attn_in['w_qkv'], 'L0_attn_w_proj': _L0_attn_in['w_proj'], 'L0_xattn_Wq': _L0_xattn_in['Wq'], 'L0_xattn_bq': _L0_xattn_in['bq'], 'L0_xattn_Wk': _L0_xattn_in['Wk'], 'L0_xattn_bk': _L0_xattn_in['bk'], 'L0_xattn_Wv': _L0_xattn_in['Wv'], 'L0_xattn_bv': _L0_xattn_in['bv'], 'L0_xattn_Wo': _L0_xattn_in['Wo'], 'L0_xattn_bo': _L0_xattn_in['bo'], 'L0_ffn_wqkv': _L0_ffn_in['wqkv'], 'L0_ffn_q_scale': _L0_ffn_in['q_scale'], 'L0_ffn_k_scale': _L0_ffn_in['k_scale'], 'L0_ffn_wo': _L0_ffn_in['wo'], 'L0_ffn_ln_g': _L0_ffn_in['ln_g'], 'L0_ffn_ln_b': _L0_ffn_in['ln_b'], 'L0_ffn_w1': _L0_ffn_in['w1'], 'L0_ffn_b1': _L0_ffn_in['b1'], 'L0_ffn_w2': _L0_ffn_in['w2'], 'L0_ffn_b2': _L0_ffn_in['b2']}

def reference(x, ctx_1024, L0_attn_w_qkv, L0_attn_w_proj, L0_xattn_Wq, L0_xattn_bq, L0_xattn_Wk, L0_xattn_bk, L0_xattn_Wv, L0_xattn_bv, L0_xattn_Wo, L0_xattn_bo, L0_ffn_wqkv, L0_ffn_q_scale, L0_ffn_k_scale, L0_ffn_wo, L0_ffn_ln_g, L0_ffn_ln_b, L0_ffn_w1, L0_ffn_b1, L0_ffn_w2, L0_ffn_b2):
    import jax
    import jax.numpy as jnp

    def _L0_attn_ref(x, w_qkv, w_proj):
        import jax, jax.numpy as jnp
        import numpy as np
        N_HEADS = 16

        def _rotate_half(t):
            shp = t.shape
            t2 = t.reshape(*shp[:-1], shp[-1] // 2, 2)
            return jnp.stack((-t2[..., 1], t2[..., 0]), axis=-1).reshape(shp)
        B, N, D = x.shape
        H = N_HEADS
        hd = D // H
        qkv = x @ w_qkv
        qkv = qkv.reshape(B, N, 3, H, hd).transpose(2, 0, 3, 1, 4)
        q, k, v = (qkv[0], qkv[1], qkv[2])
        inv_freq = 1.0 / 10000.0 ** (jnp.arange(0, hd, 2, dtype=jnp.float32) / hd)
        freqs = jnp.arange(N, dtype=jnp.float32)[:, None] * inv_freq[None, :]
        sin = jnp.repeat(jnp.sin(freqs), 2, axis=-1)[None, None]
        cos = jnp.repeat(jnp.cos(freqs), 2, axis=-1)[None, None]
        q = q * cos + _rotate_half(q) * sin
        k = k * cos + _rotate_half(k) * sin
        scale = hd ** (-0.5)
        attn = jax.nn.softmax(jnp.einsum('bhqd,bhkd->bhqk', q, k) * scale, axis=-1)
        out = jnp.einsum('bhqk,bhkd->bhqd', attn, v)
        out = out.transpose(0, 2, 1, 3).reshape(B, N, D)
        return out @ w_proj

    def _L0_xattn_ref(q, k, v, Wq, bq, Wk, bk, Wv, bv, Wo, bo):
        import jax, jax.numpy as jnp
        import numpy as np
        D_MODEL = 256
        NUM_HEADS = 16
        D_K = D_MODEL // NUM_HEADS
        B, S, D = q.shape
        H, dk = (NUM_HEADS, D_K)

        def proj(x, W, b):
            y = jnp.einsum('bsd,ed->bse', x, W) + b
            return y.reshape(B, S, H, dk).transpose(0, 2, 1, 3)
        Q = proj(q, Wq, bq)
        K = proj(k, Wk, bk)
        V = proj(v, Wv, bv)
        scores = jnp.einsum('bhqd,bhkd->bhqk', Q, K)
        attn = jax.nn.softmax(scores, axis=-1)
        out = jnp.einsum('bhqk,bhkd->bhqd', attn, V)
        out = out.transpose(0, 2, 1, 3).reshape(B, S, D)
        return jnp.einsum('bsd,ed->bse', out, Wo) + bo

    def _L0_ffn_ref(x, wqkv, q_scale, k_scale, wo, ln_g, ln_b, w1, b1, w2, b2):
        import jax, jax.numpy as jnp
        import numpy as np
        DIM = 256
        DEPTH = 2
        HEADS = 8
        DIM_HEAD = 64
        WINDOW = 128
        INNER = HEADS * DIM_HEAD
        HID = int(DIM * 4 * 2 / 3)
        B, N = (2, 2048)
        QK_SCALE = 8.0

        def shift_token(t):
            t1, t2 = jnp.split(t, 2, axis=-1)
            t2 = jnp.pad(t2, ((0, 0), (1, 0), (0, 0)))[:, :-1]
            return jnp.concatenate([t1, t2], axis=-1)

        def l2norm(t):
            return t / jnp.clip(jnp.linalg.norm(t, axis=-1, keepdims=True), 1e-12)

        def rotate_half(x):
            x1, x2 = jnp.split(x, 2, axis=-1)
            return jnp.concatenate([-x2, x1], axis=-1)

        def rotary_xpos(q, k):
            n = q.shape[-2]
            half_idx = jnp.arange(0, DIM_HEAD, 2, dtype=jnp.float32)
            inv_freq = 1.0 / 10000.0 ** (half_idx / DIM_HEAD)
            t = jnp.arange(n, dtype=jnp.float32)
            freqs = t[:, None] * inv_freq[None, :]
            freqs = jnp.concatenate([freqs, freqs], axis=-1)
            base = (half_idx + 0.4 * DIM_HEAD) / (1.4 * DIM_HEAD)
            power = (t - n // 2) / float(WINDOW // 2)
            scale = base[None, :] ** power[:, None]
            scale = jnp.concatenate([scale, scale], axis=-1)
            cos, sin = (jnp.cos(freqs), jnp.sin(freqs))
            q = q * cos * scale + rotate_half(q) * sin * scale
            k = k * cos / scale + rotate_half(k) * sin / scale
            return (q, k)

        def local_attention(q, k, v):
            b, h, n, d = q.shape
            w = n // WINDOW
            bq = q.reshape(b, h, w, WINDOW, d) * QK_SCALE
            bk = k.reshape(b, h, w, WINDOW, d)
            bv = v.reshape(b, h, w, WINDOW, d)

            def look_around(t):
                p = jnp.pad(t, ((0, 0), (0, 0), (1, 0), (0, 0), (0, 0)))
                return jnp.concatenate([p[:, :, :w], p[:, :, 1:]], axis=3)
            bk, bv = (look_around(bk), look_around(bv))
            bt = jnp.arange(n).reshape(w, WINDOW)
            btp = jnp.pad(bt, ((1, 0), (0, 0)), constant_values=-1)
            btk = jnp.concatenate([btp[:w], btp[1:]], axis=1)
            sim = jnp.einsum('bhwid,bhwjd->bhwij', bq, bk)
            i = bt[:, :, None]
            j = btk[:, None, :]
            mask = (i < j) | (i > j + WINDOW) | (j == -1)
            sim = jnp.where(mask, -jnp.finfo(sim.dtype).max, sim)
            attn = jax.nn.softmax(sim, axis=-1)
            out = jnp.einsum('bhwij,bhwjd->bhwid', attn, bv)
            return out.reshape(b, h, n, d)

        def _layer(x, wqkv, qs, ksc, wo, lg, lb, w1, b1, w2, b2):
            b, n, _ = x.shape
            h = shift_token(x)
            qkv = h @ wqkv
            q, k, v = jnp.split(qkv, 3, axis=-1)
            to_heads = lambda t: t.reshape(b, n, HEADS, DIM_HEAD).transpose(0, 2, 1, 3)
            q, k, v = (to_heads(q), to_heads(k), to_heads(v))
            q = l2norm(q) * qs
            k = l2norm(k) * ksc
            q, k = rotary_xpos(q, k)
            o = local_attention(q, k, v)
            o = o.transpose(0, 2, 1, 3).reshape(b, n, INNER)
            x = x + o @ wo
            h = shift_token(x)
            mu = h.mean(-1, keepdims=True)
            var = h.var(-1, keepdims=True)
            h = (h - mu) / jnp.sqrt(var + 1e-05) * lg + lb
            h = h @ w1 + b1
            a, g = jnp.split(h, 2, axis=-1)
            h = a * jax.nn.gelu(g, approximate=False)
            x = x + h @ w2 + b2
            return x
        for l in range(DEPTH):
            x = _layer(x, wqkv[l], q_scale[l], k_scale[l], wo[l], ln_g[l], ln_b[l], w1[l], b1[l], w2[l], b2[l])
        return x
    x = _layernorm(x + _L0_attn_ref(x, L0_attn_w_qkv, L0_attn_w_proj), axis=-1)
    x = _layernorm(x + _L0_xattn_ref(x, ctx_1024, ctx_1024, L0_xattn_Wq, L0_xattn_bq, L0_xattn_Wk, L0_xattn_bk, L0_xattn_Wv, L0_xattn_bv, L0_xattn_Wo, L0_xattn_bo), axis=-1)
    x = _layernorm(x + _L0_ffn_ref(x, L0_ffn_wqkv, L0_ffn_q_scale, L0_ffn_k_scale, L0_ffn_wo, L0_ffn_ln_g, L0_ffn_ln_b, L0_ffn_w1, L0_ffn_b1, L0_ffn_w2, L0_ffn_b2), axis=-1)
    return x

_drawn_inputs = setup_inputs


def setup_inputs(seed=0):
    import zlib

    import numpy as np

    out = dict(_drawn_inputs(seed))
    spreads = {'L0_ffn_q_scale': (1.0, 0.6),
     'L0_ffn_k_scale': (1.0, 0.6),
     'L0_ffn_ln_g': (1.0, 0.6),
     'L0_ffn_ln_b': (0.0, 0.8),
     'L0_ffn_b1': (0.0, 0.8),
     'L0_ffn_b2': (0.0, 0.1)}
    factors = {'L0_xattn_bk': 8.0}
    for name, (base, spread) in spreads.items():
        noise = np.random.default_rng([zlib.crc32(name.encode()), seed]).standard_normal(out[name].shape)
        drawn = base * np.exp(spread * noise) if base else spread * noise
        out[name] = jnp.asarray(drawn.astype(out[name].dtype))
    for name, factor in factors.items():
        out[name] = (out[name] * factor).astype(out[name].dtype)
    return out
```

```python
from contextlib import ExitStack

import numpy as np
import concourse.bass as bass
from concourse import mybir

F32 = mybir.dt.float32
F32R = mybir.dt.float32r
BF16 = mybir.dt.bfloat16
ALU = mybir.AluOpType
ACT = mybir.ActivationFunctionType
AX = mybir.AxisListType.X
P = 128
S = 512
D = 256
NEG = -3.0e38


class Queue:

    def __init__(self, name, sem):
        self.name, self.sem, self.n, self.ops, self.seen = name, sem, 0, [], {}

    def wait(self, *toks):
        for tok in toks:
            if tok is None:
                continue
            if isinstance(tok, list):
                self.wait(*tok)
                continue
            sem, value = tok
            if self.seen.get(sem.name, 0) < value:
                self.seen[sem.name] = value
                self.ops.append(lambda e, s=sem, v=value: e.wait_ge(s, v))

    def do(self, fn, *toks, sig=True):
        self.wait(*toks)
        if sig:
            self.n += 1
            self.ops.append(lambda e: fn(e).then_inc(self.sem, 1))
        else:
            self.ops.append(fn)
        return (self.sem, self.n)

    def now(self):
        return (self.sem, self.n)

    def play(self, e):
        for op in self.ops:
            op(e)


class Copies:

    def __init__(self, queue, sems):
        self.q, self.sems, self.counts, self.k = queue, sems, [0] * len(sems), 0

    def do(self, out, in_, *toks):
        k = self.k % len(self.sems)
        self.k += 1
        self.q.wait(*toks)
        if self.counts[k]:
            self.q.wait((self.sems[k], self.counts[k]))
        self.counts[k] += 16
        self.q.ops.append(lambda e, s=self.sems[k]: e.dma_start(out, in_).then_inc(s, 16))
        return (self.sems[k], self.counts[k])

    def all(self):
        return [(s, c) for s, c in zip(self.sems, self.counts) if c]


def f(ap):
    return ap.bitcast(F32)


def build(nc, t, NB, stop=None):
    with ExitStack() as ctx:
        sem = lambda n: ctx.enter_context(nc.semaphore(n))
        pe = Queue("pe", sem("s_pe"))
        act = Queue("act", sem("s_act"))
        dve = Queue("dve", sem("s_dve"))
        pool = Queue("pool", sem("s_pool"))
        sp = Queue("sp", sem("s_sp"))
        ld = Copies(sp, [sem(f"s_d{i}") for i in range(48)])
        st = Copies(pool, [sem(f"s_o{i}") for i in range(8)])
        PS = ctx.enter_context(nc.psum_tensor("PS", [P, 8, 512], F32))
        X = ctx.enter_context(nc.sbuf_tensor("X", [P, NB, 4, D], F32))
        ident = ctx.enter_context(nc.sbuf_tensor("ident", [P, P], F32))
        mhalf = ctx.enter_context(nc.sbuf_tensor("mhalf", [P, 16], F32))

        t_id = [ld.do(ident[:], t["c_ident"]),
                pool.do(lambda e: e.memset(mhalf[:], -0.5))]
        xin = [ld.do(X[:, b], t["x"][b].rearrange("(t p) d -> p t d", p=P)) for b in range(NB)]

        bank_free = [[] for _ in range(8)]
        tk = {}

        def get(*names):
            return [tk[n] for n in names if n in tk]

        def mm3(out, L, R, first, last, *toks, sig=False):
            pe.wait(*toks)
            pe.do(lambda e: e.matmul(out, L[0], R[0], start=first, stop=False), sig=False)
            pe.do(lambda e: e.matmul(out, L[0], R[1], start=False, stop=False), sig=False)
            return pe.do(lambda e: e.matmul(out, L[1], R[0], start=False, stop=last), sig=sig)

        def layernorm(src, dst, T, toks, eng_out=None):
            n = len(src)
            tk = []
            for i in range(n):
                tk.append(dve.do(lambda e, i=i: e.bn_stats(T[:, 6 * i:6 * i + 6], src[i]), *toks))
            ta = []
            for i in range(n):
                ta.append(dve.do(lambda e, i=i: e.bn_aggr(T[:, 32 + 2 * i:34 + 2 * i], T[:, 6 * i:6 * i + 6]), tk[i]))
            var = T[:, 32:32 + 2 * n].rearrange("p (n s) -> p n s", s=2)[:, :, 1]
            r = T[:, 48:48 + n]
            t1 = pool.do(lambda e: e.tensor_scalar(r, var, 1e-5, None, ALU.add), ta[-1])
            t2 = pool.do(lambda e: e.tensor_tensor(r, r, mhalf[:, 0:n], ALU.pow), t1, *t_id)
            out = []
            for i in range(n):
                out.append(dve.do(lambda e, i=i: e.tensor_scalar(
                    dst[i], src[i], T[:, 32 + 2 * i:33 + 2 * i], T[:, 48 + i:49 + i], ALU.subtract, ALU.mult), t2))
            return out[-1]

        with ExitStack() as c1:
            sb = lambda n, s, d: c1.enter_context(nc.sbuf_tensor(n, s, d))
            QS = sb("QS", [P, 2, 16, S], BF16)
            KS = sb("KS", [P, 2, 16, S], BF16)
            HL = sb("HL", [P, 3, 3, S], BF16)
            xT = sb("xT", [P, 2, 2, S], F32R)
            cst = sb("cst", [P, 2, S], F32)
            VP = sb("VP", [P, 2, 4, 16, 17], F32)
            PT = sb("PT", [P, 2, 4, S], F32)
            OT = sb("OT", [P, 2, S], F32)
            OC = sb("OC", [P, 2, S], F32)
            SM = sb("SM", [16, S], F32)
            OCr = sb("OCr", [P, 2, 2, S], F32R)
            TM = sb("TM", [P, 2, S], F32)
            MX = sb("MX", [P, 2, 4, 16], F32)
            MB = sb("MB", [P, 2, 4, 3, 8], BF16)
            MR = sb("MR", [P, 4, 8], F32)
            identb = sb("identb", [P, P], BF16)
            NM = sb("NM", [24, S], BF16)
            W = sb("W", [P, 2, 2, 5, D], F32R)
            WO = sb("WO", [P, 2, 2, 2, D], F32R)
            LNT = sb("LNT", [P, 64], F32)
            tab = sb("tab", [P, 2, S], F32)
            selR = sb("selR", [16, 2, P], F32)
            bq = sb("bq", [P, 4], F32)
            bb = sb("bb", [P, 2, D], F32)

            t_tab = ld.do(tab[:], t["c_tab"])
            t_sel = ld.do(selR[:], t["c_selR"])
            t_bq = ld.do(bq[:], t["xbqk"])
            t_bb = ld.do(bb[:], t["xbvo"])
            t_ones = []
            t_idb = dve.do(lambda e: e.tensor_copy(identb[:], ident[:]), *t_id)
            t_ones.append(dve.do(lambda e: e.memset(KS[96:P], 1.0)))
            t_ones.append(pool.do(lambda e: e.memset(VP[:], 1.0)))
            bank_free[6] = [dve.do(lambda e: e.memset(PS[:, 6, :], 0.0))]

            def load_weights(kind, free):
                wt, wo = [], []
                c = get(("cstfree",))
                x = int(kind == "x")
                for kc in range(2):
                    a = [ld.do(cst[:, j // 2, (j % 2) * D:(j % 2 + 1) * D],
                               t[f"{kind}_{name}"][kc * P:(kc + 1) * P, :], c, free)
                         for j, name in enumerate(("q", "k", "v", "o"))]
                    for j in range(4):
                        w = cst[:, j // 2, (j % 2) * D:(j % 2 + 1) * D]
                        Wh, Wl = (W[:, kc, 0, j], W[:, kc, 1, j]) if j < 3 else (WO[:, x, kc, 0], WO[:, x, kc, 1])
                        b = act.do(lambda e, Wh=Wh, w=w: e.copy(Wh, w), a, free)
                        c = dve.do(lambda e, Wl=Wl, w=w, Wh=Wh: e.tensor_tensor(Wl, w, f(Wh), ALU.subtract), a, b, free)
                        (wt if j < 3 else wo).append(c)
                        if kind == "s" and j < 2:
                            for hl in range(2):
                                s2 = W[:, kc, hl, j].rearrange("p (n two) -> p n two", two=2)
                                d2 = W[:, kc, hl, 3 + j].rearrange("p (n two) -> p n two", two=2)
                                wt.append(pool.do(lambda e, s2=s2, d2=d2: e.tensor_scalar(
                                    d2[:, :, 0], f(s2[:, :, 1]), -1.0, None, ALU.mult), c))
                                wt.append(pool.do(lambda e, s2=s2, d2=d2: e.tensor_copy(
                                    d2[:, :, 1], f(s2[:, :, 0])), c))
                tk[("cstfree",)] = [c]
                tk["W", x] = wt
                tk["WO", x] = wo

            NV = NB if stop == "self" else 0 if stop and stop[0] == "f" else 2 * NB

            def misc(fn_pe, readers):
                pe.wait(bank_free[7])
                m = fn_pe()
                bank_free[7] = readers(m)

            def chunk_transposes(vb):
                b, cross = vb % NB, vb >= NB

                def one(half):
                    def go():
                        w = get(("X", vb)) if cross else [xin[b]]

                        def mms():
                            pe.wait(w, t_id)
                            for i in range(4):
                                r = pe.do(lambda e, i=i: e.transpose(PS[:, 7, i * P:(i + 1) * P],
                                                                     X[:, b, i, half * P:(half + 1) * P], ident[:]),
                                          sig=(i == 3))
                            return r

                        def rd(m):
                            a = act.do(lambda e: e.copy(xT[:, half, 0], PS[:, 7, :]), m, get(("xTfree",)))
                            d = dve.do(lambda e: e.tensor_tensor(xT[:, half, 1], PS[:, 7, :], f(xT[:, half, 0]), ALU.subtract), a)
                            tk[("xT", vb, half)] = [a, d]
                            return [a, d]
                        misc(mms, rd)
                    return go

                def ctxt():
                    a = ld.do(cst[:], t["ctxT"][:, b * S:(b + 1) * S].rearrange("(k p) s -> p k s", p=P), get(("cstfree",)))
                    free = [pe.now()]
                    r = []
                    for kc in range(2):
                        h = act.do(lambda e, kc=kc: e.copy(xT[:, kc, 0], cst[:, kc]), a, free)
                        r.append(h)
                        r.append(dve.do(lambda e, kc=kc: e.tensor_tensor(xT[:, kc, 1], cst[:, kc], f(xT[:, kc, 0]), ALU.subtract), h, a, free))
                    tk[("cstfree",)] = list(r)
                    tk[("xT", vb, 0)] = tk[("xT", vb, 1)] = r
                return [one(0), one(1)], ctxt

            def act_in(vb):
                return get(("xT", vb, 0), ("xT", vb, 1))

            def split3(x, parts, r, ready, free):
                a = act.do(lambda e: e.copy(parts[0], x), ready, free)
                b = pool.do(lambda e: e.tensor_tensor(r, x, parts[0], ALU.subtract), a, ready, get(("rfree",)))
                c = act.do(lambda e: e.copy(parts[1], r), b)
                d = pool.do(lambda e: e.tensor_tensor(parts[2], r, parts[1], ALU.subtract), c, b)
                tk[("rfree",)] = [d]
                return [a, c, d], b

            def chunk_qk(vb, qk, tile):
                cross = vb >= NB

                def wt(j, kc, cols):
                    return (W[:, kc, 0, j, cols], W[:, kc, 1, j, cols])
                cols = slice(tile * P, (tile + 1) * P)

                def gemm(j):
                    def mms():
                        pe.wait(act_in(vb), tk["W", int(cross)])
                        for kc in range(2):
                            r = mm3(PS[:, 7, :], wt(j, kc, cols), (xT[:, kc, 0], xT[:, kc, 1]), kc == 0, kc == 1, sig=kc == 1)
                        return r
                    return mms
                hb = 2 if qk else tile
                parts = [HL[:, hb, k] for k in range(3)]

                if cross:
                    def go():
                        def rd(m):
                            bias = bq[:, 2 * qk + tile:2 * qk + tile + 1]
                            a = act.do(lambda e: e.activation(TM[:, 0], PS[:, 7, :], ACT.Identity, bias=bias), m, get(("TMfree",)), t_bq)
                            r, b = split3(TM[:, 0], parts, TM[:, 1], a, get(("HLfree", hb)))
                            tk[("TMfree",)] = r + [b]
                            tk["HL", vb, qk, tile] = r
                            return [a]
                        misc(gemm(qk), rd)
                    return [go]

                def go1():
                    def rd(m):
                        d = dve.do(lambda e: e.scalar_tensor_tensor(out=TM[:, 0], in0=PS[:, 7, :], scalar=1.0 if qk else 0.25, in1=tab[:, 0],
                                                                    op0=ALU.mult, op1=ALU.mult), m, t_tab, get(("TMfree",)))
                        tk["t1"] = d
                        return [d]
                    misc(gemm(qk), rd)

                def go2():
                    def rd(m):
                        d = dve.do(lambda e: e.scalar_tensor_tensor(out=TM[:, 1], in0=PS[:, 7, :], scalar=1.0 if qk else 0.25, in1=tab[:, 1],
                                                                    op0=ALU.mult, op1=ALU.mult), m, get(("TMfree",)))
                        x = pool.do(lambda e: e.tensor_tensor(TM[:, 0], TM[:, 0], TM[:, 1], ALU.add), d, tk["t1"])
                        r, b = split3(TM[:, 0], parts, TM[:, 1], x, get(("HLfree", hb)))
                        tk[("TMfree",)] = r + [b]
                        tk["HL", vb, qk, tile] = r
                        return [d]
                    misc(gemm(3 + qk), rd)
                return [go1, go2]

            def chunk_v(vb, half):
                cross = vb >= NB

                def go():
                    def mms():
                        pe.wait(act_in(vb), tk["W", int(cross)])
                        for i in range(2):
                            tt = 2 * half + i
                            tok = slice(tt * P, (tt + 1) * P)
                            for kc in range(2):
                                r = mm3(PS[:, 7, i * D:(i + 1) * D], (xT[:, kc, 0, tok], xT[:, kc, 1, tok]),
                                        (W[:, kc, 0, 2], W[:, kc, 1, 2]), kc == 0, kc == 1, sig=kc == 1)
                        return r

                    def rd(m):
                        src = PS[:, 7, :].rearrange("p (t h d) -> p t h d", t=2, d=16)
                        dst = VP[:, vb % 2, 2 * half:2 * half + 2, :, 0:16]
                        free = get(("VPfree", vb % 2))
                        if cross:
                            r = []
                            for i in range(2):
                                r.append(dve.do(lambda e, i=i: e.tensor_tensor(
                                    dst[:, i], src[:, i], bb[:, 0].rearrange("p (h d) -> p h d", d=16), ALU.add),
                                    m, free, t_bb, t_ones))
                        else:
                            r = [act.do(lambda e, i=i: e.copy(dst[:, i], src[:, i]), m, free, t_ones) for i in range(2)]
                        tk["V", vb, half] = r
                        return r
                    misc(mms, rd)
                return go

            def stack(vb, tile):
                s = vb % 2
                free = get(("Bdone", vb - 2, 2 * tile + 1), ("Adone", vb - 2, 2 * tile + 1))
                r = []
                for qk, T, blocks in ((0, QS, (0, 0, 0, 1, 1, 2)), (1, KS, (0, 1, 2, 0, 1, 0))):
                    hb = 2 if qk else tile
                    hs = t["hs"][s, 2 * qk + tile]
                    w = ld.do(hs, HL[:, hb], tk["HL", vb, qk, tile], get(("HSfree", s, qk, tile)))
                    tk["HLfree", hb] = [w]
                    v = hs.rearrange("(h d) a t -> a d h t", d=16)
                    rr = [ld.do(T[16 * k:16 * k + 16, s, 8 * tile:8 * tile + 8], v[a], w, free) for k, a in enumerate(blocks)]
                    tk["HSfree", s, qk, tile] = rr
                    r += rr
                for g in (2 * tile, 2 * tile + 1):
                    tk["ST", vb, g] = r

            def a_pass(vb, g, qt):
                s = vb % 2
                for p in range(2):
                    for par in range(2):
                        h = 4 * g + 2 * p + par
                        slot = 4 + par
                        pe.wait(bank_free[slot], tk["ST", vb, g])
                        m = pe.do(lambda e, h=h, slot=slot: e.matmul(
                            PS[:, slot, :], QS[0:96, s, h, qt * P:(qt + 1) * P], KS[0:96, s, h, :],
                            start=True, stop=True))
                        d = dve.do(lambda e, h=h, slot=slot: e.tensor_reduce(
                            MX[:, s, qt, h:h + 1], PS[:, slot, :], AX, ALU.max), m, get(("MXfree", vb - 2, g)))
                        bank_free[slot] = [d]
                        tk["MX", vb, g] = d
                        tk[("Adone", vb, g)] = m

            def max_rows(vb, half):
                s = vb % 2
                src = MX[:, s, :, 8 * half:8 * half + 8]
                part = [MB[:, half, :, k] for k in range(3)]
                a = dve.do(lambda e: e.tensor_copy(part[0], src), tk["MX", vb, 2 * half], tk["MX", vb, 2 * half + 1], get(("MBfree", half)))
                b = dve.do(lambda e: e.tensor_tensor(MR[:], src, part[0], ALU.subtract), a)
                c = dve.do(lambda e: e.tensor_copy(part[1], MR[:]), b)
                d = dve.do(lambda e: e.tensor_tensor(part[2], MR[:], part[1], ALU.subtract), c)
                tk[("MXfree", vb, 2 * half)] = tk[("MXfree", vb, 2 * half + 1)] = b
                out = PS[:, 7, :].bitcast(BF16)

                def mms():
                    pe.wait(d, t_idb)
                    for qt in range(4):
                        r = pe.do(lambda e, qt=qt: e.transpose(
                            out[0:24, qt * P:(qt + 1) * P], MB[:, half, qt].rearrange("p a h -> p (a h)"),
                            identb[:]), sig=qt == 3)
                    return r

                def rd(m):
                    tk[("MBfree", half)] = [m]
                    n = act.do(lambda e: e.activation(NM[:], out[0:24, 0:S], ACT.Copy, scale=-1.0), m, get(("NMfree",)))
                    r = ld.do(QS[96:99, s, 8 * half:8 * half + 8], NM[:], n, get(("Bdone", vb - 2, 2 * half + 1)))
                    tk[("NMfree",)] = [r]
                    tk["NR", vb, 2 * half] = tk["NR", vb, 2 * half + 1] = [r]
                    return [n]
                misc(mms, rd)

            def b_scores(vb, g, kt):
                s = vb % 2
                buf = kt % 2
                ex = []
                for p in range(2):
                    pe.wait(bank_free[2 * p], tk["NR", vb, g], t_ones)
                    for par in range(2):
                        h = 4 * g + 2 * p + par
                        m = pe.do(lambda e, h=h, p=p, par=par: e.matmul(
                            PS[:, 2 * p + par, :], KS[0:99, s, h, kt * P:(kt + 1) * P], QS[0:99, s, h, :],
                            start=True, stop=True), sig=par == 1)
                    tk[("Bdone", vb, g)] = m
                    a = act.do(lambda e, p=p: e.activation(PT[:, buf, 2 * p:2 * p + 2], PS[:, 2 * p:2 * p + 2, :], ACT.Exp),
                               m, get(("PTfree", buf)))
                    bank_free[2 * p] = [a]
                    ex.append(a)
                tk["PT", buf] = ex

            def pv(vb, g, kt):
                s = vb % 2
                buf = kt % 2
                pe.wait(tk["PT", buf], tk["V", vb, 0], tk["V", vb, 1])
                if kt == 0:
                    pe.wait(bank_free[6])
                for hh in range(4):
                    m = pe.do(lambda e, hh=hh: e.matmul(
                        PS[32 * hh:32 * hh + 17, 6, :], VP[:, s, kt, 4 * g + hh, :], PT[:, buf, hh, :],
                        start=kt == 0, stop=kt == 3), sig=hh == 3)
                tk[("PTfree", buf)] = [m]
                if g == 3:
                    tk[("VPfree", s)] = [m]
                if kt == 3:
                    o = g % 2
                    a = act.do(lambda e: e.copy(OT[:, o], PS[:, 6, :]), m, get(("OTfree", o)))
                    bank_free[6] = [a]
                    r = []
                    for hh in range(4):
                        h = 4 * g + hh
                        r.append(ld.do(OC[16 * (h % 8):16 * (h % 8) + 16, h // 8], OT[32 * hh:32 * hh + 16, o], a, get(("OCfree", h // 8))))
                    r.append(ld.do(SM[4 * g:4 * g + 4], OT[16:P:32, o], a, get(("SMfree",))))
                    tk[("OTfree", o)] = r
                    tk.setdefault(("OC", vb), []).extend(r)

            def chunk_out(vb):
                b, cross = vb % NB, vb >= NB

                def norm(tile):
                    def go():
                        if tile == 0:
                            tk["rc"] = dve.do(lambda e: e.reciprocal(SM[:], SM[:]), tk["OC", vb])

                        def mms():
                            return pe.do(lambda e: e.matmul(PS[:, 7, :], selR[:, tile], SM[:], start=True, stop=True),
                                         tk["rc"], t_sel)

                        def rd(m):
                            free = get(("OCrfree",))
                            d = dve.do(lambda e: e.tensor_tensor(OC[:, tile], OC[:, tile], PS[:, 7, :], ALU.mult), m, tk["OC", vb])
                            a = act.do(lambda e: e.copy(OCr[:, tile, 0], OC[:, tile]), d, free)
                            l = pool.do(lambda e: e.tensor_tensor(OCr[:, tile, 1], OC[:, tile], f(OCr[:, tile, 0]), ALU.subtract), a, d, free)
                            tk["OCr", vb, tile] = [a, l]
                            tk[("OCfree", tile)] = [l, a]
                            if tile == 1:
                                tk[("SMfree",)] = [m]
                            return [d]
                        misc(mms, rd)
                    return go

                def proj(half):
                    def go():
                        def mms():
                            pe.wait(tk["OCr", vb, 0], tk["OCr", vb, 1], tk["WO", int(cross)])
                            for i in range(2):
                                tok = slice((2 * half + i) * P, (2 * half + i + 1) * P)
                                for kc in range(2):
                                    r = mm3(PS[:, 7, i * D:(i + 1) * D], (OCr[:, kc, 0, tok], OCr[:, kc, 1, tok]),
                                            (WO[:, int(cross), kc, 0], WO[:, int(cross), kc, 1]), kc == 0, kc == 1, sig=kc == 1)
                            return r

                        def rd(m):
                            if half == 1:
                                tk[("OCrfree",)] = [m]
                            xx = X[:, b, 2 * half:2 * half + 2]
                            d = dve.do(lambda e: e.tensor_tensor(xx, PS[:, 7, :].rearrange("p (t d) -> p t d", t=2), xx, ALU.add),
                                       m, get(("Xread", vb)))
                            w = [d]
                            if cross:
                                for i in range(2):
                                    w.append(pool.do(lambda e, i=i: e.tensor_tensor(
                                        X[:, b, 2 * half + i], X[:, b, 2 * half + i], bb[:, 1], ALU.add), d, t_bb))
                            l = layernorm([X[:, b, 2 * half + i] for i in range(2)], [X[:, b, 2 * half + i] for i in range(2)], LNT, w)
                            tk.setdefault(("X", vb + NB), []).append(l)
                            if cross:
                                r = st.do(t["x2s"][b, :, 2 * half:2 * half + 2, :], xx, l)
                                tk.setdefault(("x2s", b), []).append(r)
                            return [d]
                        misc(mms, rd)
                    return go
                return [norm(0), norm(1), proj(0), proj(1)]

            load_weights("s", [])

            def p_chunks(vb):
                tr, ctxt = chunk_transposes(vb)
                q = chunk_qk(vb, 0, 0) + chunk_qk(vb, 0, 1)
                k0, k1 = chunk_qk(vb, 1, 0), chunk_qk(vb, 1, 1)
                return tr + q + ([ctxt] if vb >= NB else []) + k0, k1

            for step in range(-1, NV + 2):
                vbA, vbB, vbP, vbO = step, step - 1, step + 1, step - 2
                hasA, hasB, hasP, hasO = 0 <= vbA < NV, 0 <= vbB < NV, vbP < NV, 0 <= vbO < NV
                first, second = p_chunks(vbP) if hasP else ([], [])
                slots = [[] for _ in range(16)]
                if hasA:
                    slots[0] = [chunk_v(vbA, 0)]
                    slots[1] = [chunk_v(vbA, 1), lambda: tk.__setitem__(("xTfree",), [pe.now()])]
                if hasP and vbP == NB:
                    slots[1].append(lambda: load_weights("x", [pe.now()]))
                for i, c in enumerate(chunk_out(vbO) if hasO else []):
                    slots[(1, 3, 6, 10)[i]].append(c)
                for i, c in enumerate(first):
                    slots[2 + min(6 * i // len(first), 5)].append(c)
                for i, c in enumerate(second):
                    slots[9 + 3 * i].append(c)
                for g in range(4):
                    for k in range(4):
                        if hasA:
                            a_pass(vbA, g, k)
                        if hasB:
                            b_scores(vbB, g, k)
                        if k == 0 and g == 2 and hasA:
                            max_rows(vbA, 0)
                        if hasB and (k or g):
                            pv(vbB, g if k else g - 1, (k - 1) % 4)
                        for c in slots[4 * g + k]:
                            c()
                    if g == 3 and hasB:
                        pv(vbB, 3, 3)
                    if hasP and g in (1, 3):
                        stack(vbP, g // 2)
                if hasA:
                    max_rows(vbA, 1)
                if stop in ("att", "self") and step == NV + 1:
                    for b in range(NB):
                        st.do(t["out"][b].rearrange("(t p) d -> p t d", p=P), X[:, b], tk[("X", NV + b)])
        if stop not in ("att", "self"):
            for b in range(NB):
                if NV:
                    tk["FX", 0, b] = tk["X", 2 * NB + b]
                else:
                    tk["FX", 0, b] = [xin[b]]
                    st.do(t["x2s"][b], X[:, b], xin[b])
            ffn(nc, ctx, t, NB, stop, dict(pe=pe, act=act, dve=dve, pool=pool, sp=sp, ld=ld, st=st, PS=PS, X=X,
                                           ident=ident, mhalf=mhalf, t_id=t_id, tk=tk, mm3=mm3, get=get,
                                           layernorm=layernorm))
        queues_end(nc, ctx, pe, act, dve, pool, sp, ld, st)


def ffn(nc, ctx, t, NB, stop, g):
    pe, act, dve, pool, sp, ld, st = (g[n] for n in ("pe", "act", "dve", "pool", "sp", "ld", "st"))
    PS, X, ident, mhalf, t_id, tk, mm3, get, layernorm = (g[n] for n in (
        "PS", "X", "ident", "mhalf", "t_id", "tk", "mm3", "get", "layernorm"))
    engines = (pe, act, dve, pool, sp)
    free = [[] for _ in range(8)]

    def barrier():
        all_ = [q.now() for q in (pe, act, dve, pool)] + ld.all() + st.all()
        for q in engines:
            q.wait(all_)

    barrier()
    sb = lambda n, s, d: ctx.enter_context(nc.sbuf_tensor(n, s, d))
    WQ = sb("WQ", [P, 2, 2, 1536], F32R)
    WOF = sb("WOF", [P, 4, 2, D], F32R)
    W1 = sb("W1", [P, 2, 2, 1536], F32R)
    W2 = sb("W2", [P, 6, 2, D], F32R)
    rot = sb("rot", [P, 4, 4, 64], F32)
    mask = sb("mask", [P, 2, 256], BF16)
    identb = sb("identbf", [P, P], BF16)
    cols = sb("cols", [P, 2, 16], F32)
    b2 = sb("b2", [P, 2, D], F32)
    stage = sb("stage", [P, 2, 768], F32)
    t_cols = [ld.do(cols[:], t["f_cols"]), ld.do(b2[:], t["f_b2"])]
    t_idb = [dve.do(lambda e: e.tensor_copy(identb[:], ident[:]))]
    k_stage = [0]
    sfree = [[], []]

    def split_load(dsts, src, ready):
        s = k_stage[0] % 2
        k_stage[0] += 1
        n = src.shape[-1]
        a = ld.do(stage[:, s, 0:n], src, sfree[s])
        h = act.do(lambda e: e.copy(dsts[0], stage[:, s, 0:n]), a, ready)
        l = pool.do(lambda e: e.tensor_tensor(dsts[1], stage[:, s, 0:n], f(dsts[0]), ALU.subtract), h, a, ready)
        sfree[s] = [h, l]
        return [h, l]

    def load_attn(L, ready):
        r = []
        for kc in range(2):
            for c in range(2):
                r += split_load([WQ[:, kc, i, 768 * c:768 * c + 768] for i in range(2)],
                                t["f_wqkv"][L, kc * P:(kc + 1) * P, 768 * c:768 * c + 768], ready)
        for kc in range(4):
            r += split_load([WOF[:, kc, i] for i in range(2)], t["f_wo"][L, kc * P:(kc + 1) * P, :], ready)
        tk["WA", L] = r

    def load_mlp(L, ready):
        r = []
        for kc in range(2):
            for c in range(2):
                r += split_load([W1[:, kc, i, 768 * c:768 * c + 768] for i in range(2)],
                                t["f_w1"][L, kc * P:(kc + 1) * P, c, :], ready)
        for kc in range(6):
            r += split_load([W2[:, kc, i] for i in range(2)], t["f_w2"][L, kc * P:(kc + 1) * P, :], ready)
        tk["WM", L] = r

    def xtokens(L, b):
        return get(("FX", L, b))

    def attention(L):
        with ExitStack() as c2:
            s2 = lambda n, s, d: c2.enter_context(nc.sbuf_tensor(f"{n}{L}", s, d))
            XT = s2("XT", [P, 2, 2, 2, S + 2], F32R)
            qT = s2("qT", [P, 2, 4, 2, P], F32R)
            kT = s2("kT", [P, 4, 2, S], F32R)
            V = s2("V", [P, 4, S], F32)
            SQ = s2("SQ", [P, 2, S], F32)
            RA = s2("RA", [P, 2, S], F32)
            RB = s2("RB", [P, 2, S], F32)
            RI = s2("RI", [P, 2, 8], F32)
            PB = s2("PB", [P, 2, 8, 256], F32)
            PTB = s2("PTB", [P, 4, 4, P], F32)
            NM = s2("NMf", [P, 2, 8], F32)
            SUM = s2("SUM", [P, 2, 8], F32)
            RC = s2("RC", [P, 8], F32)
            O = s2("O", [P, S], F32)
            OTr = s2("OTr", [P, 2, 4, P], F32R)
            qks = s2("qks", [P, 4, 64], F32)
            mk = s2("mk", [P, 256], F32)
            dma = [ld.do(qks[:], t["f_qks"][:, L]), ld.do(mk[:], t["c_mask"]), ld.do(rot[:], t["c_rot"])]
            t_mask = [dve.do(lambda e, i=i: e.tensor_copy(mask[:, i], mk[:]), dma) for i in range(2)] + t_idb
            t_rot = [dve.do(lambda e, j=j: e.tensor_tensor(
                rot[:, j], rot[:, j], qks[:, j:j + 1, :].broadcast_to([P, 4, 64]), ALU.mult), dma) for j in range(4)]
            t_z = [dve.do(lambda e: e.memset(f(XT[:, :, 1, :, 0:1]), 0.0))]
            loc = {}

            def lg(*names):
                return [loc[n] for n in names if n in loc]

            def misc(mms, rd):
                pe.wait(free[2])
                free[2] = rd(mms())

            def xt(b, half):
                bp = b % 2

                def mms():
                    pe.wait(xtokens(L, b), t_id)
                    for i in range(4):
                        r = pe.do(lambda e, i=i: e.transpose(PS[:, 2, i * P:(i + 1) * P], X[:, b, i, half * P:(half + 1) * P],
                                                             ident[:]), sig=i == 3)
                    return r

                def rd(m):
                    h, l = (XT[:, bp, half, k, half:half + S] for k in range(2))
                    w = lg(("XTread", b - 2))
                    a = act.do(lambda e: e.copy(h, PS[:, 2, :]), m, w)
                    d = dve.do(lambda e: e.tensor_tensor(l, PS[:, 2, :], f(h), ALU.subtract), a, m, w)
                    loc["XT", b, half] = [a, d]
                    return [a, d]
                misc(mms, rd)

            def gemm(u, part, bank):
                b, i = divmod(u, 4)
                pe.wait(loc["XT", b, 0], loc["XT", b, 1], t_z, tk["WA", L], free[bank])
                for kc in range(2):
                    r = mm3(PS[:, bank, :], [XT[:, b % 2, kc, k, i * P:(i + 1) * P] for k in range(2)],
                            [WQ[:, kc, k, part * S:(part + 1) * S] for k in range(2)], kc == 0, kc == 1, sig=kc == 1)
                if part == 2 and i == 3:
                    loc["XTread", b] = r
                return r

            def qk_post(u, part, bank, m):
                i = u % 4
                ps = PS[:, bank, :]
                psh = ps.rearrange("p (h d) -> p h d", d=64)
                w = lg(("Rfree", part))
                a0 = act.do(lambda e: e.activation(SQ[:, part], ps, ACT.Square), m, lg(("SQfree", part)))
                d1 = dve.do(lambda e: e.tensor_tensor(RA[:, part].rearrange("p (h d) -> p h d", d=64), psh,
                                                      rot[:, 2 * part, i:i + 1, :].broadcast_to([P, 8, 64]), ALU.mult), a0, w, t_rot)
                rb = RB[:, part].rearrange("p (h d) -> p h d", d=64)
                d2 = [dve.do(lambda e, o=o: e.tensor_tensor(
                    rb[:, :, o:o + 32], psh[:, :, 32 - o:64 - o],
                    rot[:, 2 * part + 1, i:i + 1, o:o + 32].broadcast_to([P, 8, 32]), ALU.mult), a0, w, t_rot) for o in (0, 32)]
                d3 = dve.do(lambda e: e.tensor_reduce(RI[:, part], SQ[:, part].rearrange("p (h d) -> p h d", d=64), AX, ALU.add),
                            a0, lg(("RIfree", part)))
                loc["SQfree", part] = [d3]
                p1 = pool.do(lambda e: e.tensor_scalar(RI[:, part], RI[:, part], 1e-24, None, ALU.max), d3)
                p2 = pool.do(lambda e: e.tensor_tensor(RI[:, part], RI[:, part], mhalf[:, 0:8], ALU.pow), p1)
                p3 = pool.do(lambda e: e.tensor_tensor(RA[:, part], RA[:, part], RB[:, part], ALU.add), d1, d2)
                ra = RA[:, part].rearrange("p (h d) -> p h d", d=64)
                p4 = pool.do(lambda e: e.tensor_tensor(ra, ra, RI[:, part].unsqueeze(2).broadcast_to([P, 8, 64]), ALU.mult), p3, p2)
                loc["RIfree", part] = [p4]
                loc["R", u, part] = [p4]
                free[bank] = [a0, d1] + d2

            def qkt(u, part):
                b, i = divmod(u, 4)

                def mms():
                    pe.wait(loc["R", u, part])
                    for c in range(4):
                        r = pe.do(lambda e, c=c: e.transpose(PS[:, 2, c * P:(c + 1) * P], RA[:, part, c * P:(c + 1) * P], ident[:]),
                                  sig=c == 3)
                    loc["Rfree", part] = [r]
                    return r

                def rd(m):
                    src = PS[:, 2, :].rearrange("p (c t) -> p c t", t=P)
                    if part == 0:
                        h, l = (qT[:, u % 2, :, k] for k in range(2))
                        w = lg(("Sdone", u - 2))
                    else:
                        h, l = (kT[:, :, k, i * P:(i + 1) * P] for k in range(2))
                        w = lg(("Sdone", u - 3))
                    a = act.do(lambda e: e.copy(h, src), m, w)
                    d = dve.do(lambda e: e.tensor_tensor(l, src, f(h), ALU.subtract), a, m, w)
                    loc["T", u, part] = [a, d]
                    return [a, d]
                misc(mms, rd)

            def heads(hp):
                h = 4 * (hp // 2) + hp % 2
                return (h, h + 2)

            def scores(u, hp):
                b, i = divmod(u, 4)
                bank = 4 + hp % 2
                k0 = 0 if i else P
                pe.wait(free[bank], t_mask, loc["T", u, 0], loc["T", u, 1])
                out = PS[:, bank, :].rearrange("p (h k) -> p h k", h=2)
                pe.do(lambda e: e.matmul(out[:, :, k0:], identb[:], mask[:, :, k0:], start=True, stop=False,
                                         skip_group_check=True), sig=False)
                keys = slice((i - 1) * P if i else 0, (i + 1) * P)
                for x, y in ((0, 0), (0, 1), (1, 0)):
                    for h in range(2):
                        hh = heads(hp)[h]
                        rows = slice(64 * (hh % 2), 64 * (hh % 2) + 64)
                        m = pe.do(lambda e, h=h, hh=hh, rows=rows, x=x, y=y: e.matmul(
                            out[:, h, k0:], qT[rows, u % 2, hh // 2, x], kT[rows, hh // 2, y, keys], start=False, stop=x == 1,
                            skip_group_check=True), sig=h == 1 and x == 1)
                if hp == 3:
                    loc["Sdone", u] = [m]
                d = dve.do(lambda e: e.tensor_reduce(NM[:, u % 2, heads(hp)[0]:heads(hp)[1] + 1:2], out[:, :, k0:], AX, ALU.max, negate=True),
                           m, lg(("E", u - 2)))
                ex = []
                for h in range(2):
                    hh = heads(hp)[h]
                    ex.append(act.do(lambda e, h=h, hh=hh: e.activation(
                        PB[:, u % 2, hh, k0:], out[:, h, k0:], ACT.Exp, bias=NM[:, u % 2, hh:hh + 1],
                        accum_out=SUM[:, u % 2, hh:hh + 1]), d, m, lg(("PBfree", u - 2), ("SUMfree", u - 2))))
                free[bank] = ex
                loc["E", u] = loc["E", u, hp] = ex

            def ptrans(u, hp):
                i = u % 4
                bank = 6 + hp % 2
                pe.wait(free[bank], loc["E", u, hp])
                js = (0, 1) if i else (1,)
                for h in range(2):
                    for j in js:
                        m = pe.do(lambda e, h=h, j=j: e.transpose(
                            PS[:, bank, (2 * h + j) * P:(2 * h + j + 1) * P],
                            PB[:, u % 2, heads(hp)[h], j * P:(j + 1) * P], ident[:]), sig=h == 1 and j == 1)
                src = PS[:, bank, :].rearrange("p (h j q) -> p h j q", h=2, j=2)
                dst = PTB[:, hp].rearrange("p (h j) q -> p h j q", h=2)
                if i == 0:
                    src, dst = src[:, :, 1], dst[:, :, 1]
                w = lg(("PV", u - 1, hp))
                if hp % 2:
                    a = dve.do(lambda e: e.tensor_copy(dst, src), m, w)
                else:
                    a = act.do(lambda e: e.copy(dst, src), m, w)
                free[bank] = [a]
                loc["PT", u, hp] = [a]
                if hp == 3:
                    loc["PBfree", u] = [m]

            def pv(u, hp):
                b, i = divmod(u, 4)
                pe.wait(loc["PT", u, hp], loc["V", u])
                if hp == 0:
                    pe.wait(free[3])
                js = (0, 1) if i else (1,)
                for h in range(2):
                    hh = heads(hp)[h]
                    for j in js:
                        m = pe.do(lambda e, h=h, j=j, hh=hh: e.matmul(
                            PS[:, 3, hh * 64:hh * 64 + 64], PTB[:, hp, 2 * h + j], V[:, i - 1 + j, hh * 64:hh * 64 + 64],
                            start=j == js[0], stop=j == 1), sig=h == 1 and j == 1)
                loc["PV", u, hp] = [m]
                if hp == 3:
                    loc["Vfree", u] = [m]
                    r = dve.do(lambda e: e.reciprocal(RC[:], SUM[:, u % 2]), loc["E", u], lg(("Oread",)))
                    loc["SUMfree", u] = [r]
                    d = dve.do(lambda e: e.tensor_tensor(
                        O[:].rearrange("p (h d) -> p h d", d=64), PS[:, 3, :].rearrange("p (h d) -> p h d", d=64),
                        RC[:].unsqueeze(2).broadcast_to([P, 8, 64]), ALU.mult), m, r, lg(("Oread",)))
                    free[3] = [d]
                    loc["O", u] = [d]

            def ot(u):
                def mms():
                    pe.wait(loc["O", u])
                    for c in range(4):
                        r = pe.do(lambda e, c=c: e.transpose(PS[:, 2, c * P:(c + 1) * P], O[:, c * P:(c + 1) * P], ident[:]),
                                  sig=c == 3)
                    loc[("Oread",)] = [r]
                    return r

                def rd(m):
                    src = PS[:, 2, :].rearrange("p (c t) -> p c t", t=P)
                    w = lg(("OTfree",))
                    a = act.do(lambda e: e.copy(OTr[:, 0], src), m, w)
                    d = dve.do(lambda e: e.tensor_tensor(OTr[:, 1], src, f(OTr[:, 0]), ALU.subtract), a, m, w)
                    loc["OT", u] = [a, d]
                    return [a, d]
                misc(mms, rd)

            def wo(u):
                b, i = divmod(u, 4)

                def mms():
                    pe.wait(loc["OT", u])
                    for c in range(4):
                        r = mm3(PS[:, 2, 0:D], [OTr[:, k, c] for k in range(2)], [WOF[:, c, k] for k in range(2)],
                                c == 0, c == 3, sig=c == 3)
                    loc[("OTfree",)] = [r]
                    return r

                def rd(m):
                    d = dve.do(lambda e: e.tensor_tensor(X[:, b, i], PS[:, 2, 0:D], X[:, b, i], ALU.add), m)
                    tk.setdefault(("FA", L, b), []).append(d)
                    return [d]
                misc(mms, rd)

            NU = 4 * NB
            for h in range(2):
                xt(0, h)
            for n in range(-1, NU + 2):
                A, B, C, Q = n, n - 1, n - 2, n + 1
                hA, hB, hC, hQ = 0 <= A < NU, 0 <= B < NU, 0 <= C < NU, Q < NU
                if hA: scores(A, 0)
                if hB: ptrans(B, 0)
                if hQ: qk_post(Q, 0, 0, gemm(Q, 0, 0))
                if hC: ot(C)
                if hA: scores(A, 1)
                if hQ: qk_post(Q, 1, 1, gemm(Q, 1, 1))
                if hB: ptrans(B, 1); pv(B, 0)
                if hC: wo(C)
                if hA: scores(A, 2)
                if hQ:
                    m = gemm(Q, 2, 0)
                    v = act.do(lambda e, Q=Q: e.copy(V[:, Q % 4], PS[:, 0, :]), m, lg(("Vfree", Q - 3)))
                    free[0] = [v]
                    loc["V", Q] = [v]
                if hB: ptrans(B, 2); pv(B, 1)
                if hQ:
                    qkt(Q, 0)
                if hA: scores(A, 3)
                if hQ and Q % 4 in (1, 2) and Q // 4 + 1 < NB:
                    xt(Q // 4 + 1, Q % 4 - 1)
                if hB: ptrans(B, 3); pv(B, 2)
                if hQ:
                    qkt(Q, 1)
                if hB: pv(B, 3)
            barrier()

    def mlp(L):
        with ExitStack() as c2:
            s2 = lambda n, s, d: c2.enter_context(nc.sbuf_tensor(f"{n}{L}", s, d))
            XS = s2("XS", [P, 2, 4, P], F32)
            HN = s2("HN", [P, 2, 4, D], F32)
            HT = s2("HT", [P, 2, 2, 2, S], F32R)
            TT = s2("TT", [P, S], F32)
            G = s2("G", [P, 2, S], F32)
            U = s2("U", [P, 2, S], F32)
            UR = s2("UR", [P, 2, 6, 2, S], F32R)
            ST = s2("ST", [P, 2, 128], F32)
            Y = s2("Y", [P, 4, D], F32) if L == 1 else None
            LNT = s2("LNT", [P, 64], F32)
            loc = {}
            t_z = [dve.do(lambda e: e.memset(XS[0:1, :, 0, :], 0.0))]

            def lg(*names):
                return [loc[n] for n in names if n in loc]

            def shift(b):
                s = b % 2
                w = [get(("FA", L, b)), lg(("XSfree", b - 2))]
                loc["XS", b] = [ld.do(XS[1:P, s], X[0:P - 1, b, :, P:D], w), ld.do(XS[0:1, s, 1:4], X[P - 1:P, b, 0:3, P:D], w)]

            def norm(b):
                s = b % 2
                w = loc["XS", b] + t_z
                T = ST[:, s]
                tr = lg(("HNfree", b - 2))
                ta = []
                for i in range(4):
                    x = dve.do(lambda e, i=i: e.bn_stats(T[:, 12 * i:12 * i + 6], X[:, b, i, 0:P]), w, lg(("STfree", b - 2)))
                    y = dve.do(lambda e, i=i: e.bn_stats(T[:, 12 * i + 6:12 * i + 12], XS[:, s, i]), w)
                    ta.append((x, y))
                for i in range(4):
                    z = dve.do(lambda e, i=i: e.bn_aggr(T[:, 64 + 2 * i:66 + 2 * i], T[:, 12 * i:12 * i + 12]), *ta[i])
                var = T[:, 64:72].rearrange("p (n s) -> p n s", s=2)[:, :, 1]
                r = T[:, 80:84]
                t1 = pool.do(lambda e: e.tensor_scalar(r, var, 1e-5, None, ALU.add), z)
                t2 = pool.do(lambda e: e.tensor_tensor(r, r, mhalf[:, 0:4], ALU.pow), t1)
                o = []
                for half, src in ((0, lambda i: X[:, b, i, 0:P]), (1, lambda i: XS[:, s, i])):
                    for i in range(4):
                        o.append(dve.do(lambda e, i=i, half=half, src=src: e.tensor_scalar(
                            HN[:, s, i, half * P:(half + 1) * P], src(i), T[:, 64 + 2 * i:65 + 2 * i], T[:, 80 + i:81 + i],
                            ALU.subtract, ALU.mult), t2, z, tr))
                loc["HN", b] = o
                loc["XSfree", b] = loc["STfree", b] = o

            def ht(b, half, bank):
                s = b % 2
                pe.wait(free[bank], loc["HN", b])
                for i in range(4):
                    m = pe.do(lambda e, i=i: e.transpose(PS[:, bank, i * P:(i + 1) * P], HN[:, s, i, half * P:(half + 1) * P],
                                                         ident[:]), sig=i == 3)
                if half == 1:
                    loc["HNfree", b] = [m]
                d = dve.do(lambda e: e.tensor_scalar(TT[:], PS[:, bank, :], cols[:, L, 12 + half:13 + half],
                                                     cols[:, L, 14 + half:15 + half], ALU.mult, ALU.add), m, t_cols, lg(("TTfree",)))
                free[bank] = [d]
                w = lg(("W1done", b - 2))
                a = act.do(lambda e: e.copy(HT[:, s, half, 0], TT[:]), d, w)
                l = pool.do(lambda e: e.tensor_tensor(HT[:, s, half, 1], TT[:], f(HT[:, s, half, 0]), ALU.subtract), a, d, w)
                loc[("TTfree",)] = [a, l]
                loc["HT", b, half] = [a, l]

            def w1(b, c):
                s = b % 2
                banks = (2 * (c % 2), 2 * (c % 2) + 1)
                ms = []
                pe.wait(loc["HT", b, 0], loc["HT", b, 1], tk["WM", L])
                for ag in (1, 0):
                    bank = banks[ag]
                    pe.wait(free[bank])
                    for kc in range(2):
                        m = mm3(PS[:, bank, :], [W1[:, kc, k, ag * 768 + c * P:ag * 768 + (c + 1) * P] for k in range(2)],
                                [HT[:, s, kc, k] for k in range(2)], kc == 0, kc == 1, sig=kc == 1)
                    ms.append(m)
                if c == 5:
                    loc["W1done", b] = [m]
                q = c % 2
                a = act.do(lambda e: e.activation(G[:, q], PS[:, banks[1], :], ACT.Gelu, bias=cols[:, L, 6 + c:7 + c]),
                           ms[0], t_cols, lg(("Gfree", q)))
                d = dve.do(lambda e: e.scalar_tensor_tensor(out=U[:, q], in0=PS[:, banks[0], :], scalar=cols[:, L, c:c + 1],
                                                            in1=G[:, q], op0=ALU.add, op1=ALU.mult), ms[1], a, lg(("Ufree", q)))
                free[banks[1]], free[banks[0]] = [a], [d]
                loc["Gfree", q] = [d]
                w = lg(("URfree", b - 2))
                h = act.do(lambda e: e.copy(UR[:, s, c, 0], U[:, q]), d, w)
                l = pool.do(lambda e: e.tensor_tensor(UR[:, s, c, 1], U[:, q], f(UR[:, s, c, 0]), ALU.subtract), h, d, w)
                loc["Ufree", q] = [h, l]
                loc.setdefault(("U", b), []).extend([h, l])

            def w2(b, i):
                s = b % 2
                bank = 4 + i % 2
                if L == 1 and i == 0:
                    loc["Y", b] = [ld.do(Y[:], t["x2s"][b], lg(("Yfree", b - 1)))]
                pe.wait(free[bank], loc["U", b])
                for c in range(6):
                    m = mm3(PS[:, bank, 0:D], [UR[:, s, c, k, i * P:(i + 1) * P] for k in range(2)],
                            [W2[:, c, k] for k in range(2)], c == 0, c == 5, sig=c == 5)
                if i == 3:
                    loc["URfree", b] = [m]
                d = dve.do(lambda e: e.tensor_tensor(X[:, b, i], PS[:, bank, 0:D], X[:, b, i], ALU.add), m, loc["HN", b], loc["XS", b])
                free[bank] = [d]
                p = pool.do(lambda e: e.tensor_tensor(X[:, b, i], X[:, b, i], b2[:, L], ALU.add), d, t_cols)
                tk.setdefault(("FX", L + 1, b), []).append(p)
                if L == 1:
                    p2 = pool.do(lambda e: e.tensor_tensor(X[:, b, i], X[:, b, i], Y[:, i], ALU.add), p, loc["Y", b])
                    loc["Yp", b, i] = p2
                    if i == 3:
                        w = [loc["Yp", b, j] for j in range(4)]
                        l = layernorm([X[:, b, j] for j in range(4)], [X[:, b, j] for j in range(4)], LNT, w)
                        loc["Yfree", b] = [p2]
                        st.do(t["out"][b].rearrange("(t p) d -> p t d", p=P), X[:, b], l)

            shift(0)
            norm(0)
            if NB > 1:
                shift(1)
            ht(0, 0, 6)
            ht(0, 1, 7)
            for b in range(NB + 1):
                for c in range(6):
                    if b < NB:
                        w1(b, c)
                    if b + 1 < NB and c == 1:
                        norm(b + 1)
                        if b + 2 < NB:
                            shift(b + 2)
                    if b + 1 < NB and c in (4, 5):
                        ht(b + 1, c - 4, 6 + c - 4)
                    if b >= 1 and c in (1, 2, 3, 4):
                        w2(b - 1, c - 1)
            barrier()

    for L in range(2):
        if L == 0:
            load_attn(0, [])
            load_mlp(0, [])
        attention(L)
        if stop == f"fa{L}":
            for b in range(NB):
                st.do(t["out"][b].rearrange("(t p) d -> p t d", p=P), X[:, b], tk["FA", L, b])
            return
        if L == 0:
            load_attn(1, [])
        mlp(L)
        if stop == f"fm{L}":
            for b in range(NB):
                st.do(t["out"][b].rearrange("(t p) d -> p t d", p=P), X[:, b], tk["FX", L + 1, b])
            return
        if L == 0:
            load_mlp(1, [])


def queues_end(nc, ctx, pe, act, dve, pool, sp, ld, st):
    sp.wait(*st.all(), *ld.all())
    block = ctx.enter_context(nc.Block())
    block.tensor(pe.play)
    block.scalar(act.play)
    block.vector(dve.play)
    block.gpsimd(pool.play)
    block.sync(sp.play)


def constants():
    n = np.arange(S, dtype=np.float32)
    inv = (1.0 / np.power(np.float32(10000.0), np.arange(0, 16, 2, dtype=np.float32) / np.float32(16))).astype(np.float32)
    fr = n[:, None] * inv[None, :]
    sin, cos = np.sin(fr), np.cos(fr)
    tab = np.zeros((P, 2, S), np.float32)
    for r in range(P):
        tab[r, 0], tab[r, 1] = cos[:, r % 16 // 2], sin[:, r % 16 // 2]
    selR = np.zeros((16, 2, P), np.float32)
    for h in range(16):
        selR[h, h // 8, 16 * (h % 8):16 * (h % 8) + 16] = 1.0
    hi = np.arange(0, 64, 2, dtype=np.float32)
    inv = (np.float32(1.0) / np.power(np.float32(10000.0), hi / np.float32(64))).astype(np.float32)
    fr = n[:, None] * inv[None, :]
    base = (hi + np.float32(0.4 * 64)) / np.float32(1.4 * 64)
    scale = np.power(base[None, :], ((n - 256) / np.float32(64))[:, None]).astype(np.float32)
    cos, sin = np.cos(fr), np.sin(fr)
    rot = np.stack([np.concatenate(v, 1) for v in (
        (cos * scale * 8, cos * scale * 8), (-sin * scale * 8, sin * scale * 8),
        (cos / scale, cos / scale), (-sin / scale, sin / scale))]).astype(np.float32)
    rot = np.ascontiguousarray(rot.reshape(4, 4, P, 64).transpose(2, 0, 1, 3))
    q, k = np.arange(P)[:, None], np.arange(256)[None, :]
    mask = np.where((k < P) & (k < q) | (k >= P) & (k - P > q), np.float32(NEG), np.float32(0)).astype(np.float32)
    return {"c_rot": rot, "c_mask": mask, "c_ident": np.eye(P, dtype=np.float32), "c_tab": tab, "c_selR": selR}


def layout(inputs, NB=8):
    c = np.ascontiguousarray
    i = {k: np.asarray(v) for k, v in inputs.items()}
    a = constants()
    a["x"] = c(i["x"][:NB])
    a["ctxT"] = c(i["ctx_1024"][:NB].reshape(NB * S, D).T)
    for j, n in enumerate("qkv"):
        a["s_" + n] = c(i["L0_attn_w_qkv"][:, j * D:(j + 1) * D])
    a["s_o"] = c(i["L0_attn_w_proj"])
    for n in "qkvo":
        a["x_" + n] = c(i["L0_xattn_W" + n].T)
    a["xbqk"] = c(np.concatenate([i["L0_xattn_bq"].reshape(2, P), i["L0_xattn_bk"].reshape(2, P)]).T)
    a["xbvo"] = c(np.stack([np.broadcast_to(i["L0_xattn_b" + n], (P, D)) for n in "vo"], 1))
    qs, ks = i["L0_ffn_q_scale"], i["L0_ffn_k_scale"]
    sw = lambda v: np.concatenate([v[:, 32:], v[:, :32]], 1)
    qk = np.stack([qs, sw(qs), ks, sw(ks)], 1)
    a["f_qks"] = c(np.broadcast_to(qk[None], (P, 2, 4, 64)))
    a["f_wqkv"] = c(i["L0_ffn_wqkv"])
    a["f_wo"] = c(i["L0_ffn_wo"])
    H = i["L0_ffn_w2"].shape[1]
    w1 = np.zeros((2, D, 2, 768), np.float32)
    w1[..., :H] = i["L0_ffn_w1"].reshape(2, D, 2, H)
    w2 = np.zeros((2, 768, D), np.float32)
    w2[:, :H] = i["L0_ffn_w2"]
    b1 = np.zeros((2, 2, 768), np.float32)
    b1[..., :H] = i["L0_ffn_b1"].reshape(2, 2, H)
    cols = np.concatenate([b1.reshape(2, 12, P), i["L0_ffn_ln_g"].reshape(2, 2, P), i["L0_ffn_ln_b"].reshape(2, 2, P)], 1)
    a["f_w1"], a["f_w2"] = w1, w2
    a["f_cols"] = c(cols.transpose(2, 0, 1))
    a["f_b2"] = c(np.broadcast_to(i["L0_ffn_b2"][None], (P, 2, D)))
    return a


def kernel(**inputs):
    import concourse.bacc as bacc
    from concourse.bass_utils import run_bass_kernel_spmd

    arrays = layout(inputs)
    nc = bacc.Bacc("TRN2", target_bir_lowering=False, num_devices=1)
    t = {k: nc.dram_tensor(k, a.shape, mybir.dt.from_np(a.dtype), kind="ExternalInput").ap() for k, a in arrays.items()}
    t["out"] = nc.dram_tensor("out", (8, S, D), F32, kind="ExternalOutput").ap()
    t["x2s"] = nc.dram_tensor("x2s", (8, P, 4, D), F32, kind="Internal").ap()
    t["hs"] = nc.dram_tensor("hs", (2, 4, P, 3, S), BF16, kind="Internal").ap()
    build(nc, t, 8)
    r = run_bass_kernel_spmd(nc, [arrays], core_ids=[0])
    return r.results[0]["out"]
```

```python
from contextlib import ExitStack

import numpy as np
import concourse.bass as bass
from concourse import mybir

F32 = mybir.dt.float32
F32R = mybir.dt.float32r
BF16 = mybir.dt.bfloat16
ALU = mybir.AluOpType
ACT = mybir.ActivationFunctionType
AX = mybir.AxisListType.X
P = 128
S = 512
D = 256
NEG = -3.0e38


class Queue:

    def __init__(self, name, sem):
        self.name, self.sem, self.n, self.ops, self.seen = name, sem, 0, [], {}

    def wait(self, *toks):
        for tok in toks:
            if tok is None:
                continue
            if isinstance(tok, list):
                self.wait(*tok)
                continue
            sem, value = tok
            if self.seen.get(sem.name, 0) < value:
                self.seen[sem.name] = value
                self.ops.append(lambda e, s=sem, v=value: e.wait_ge(s, v))

    def do(self, fn, *toks, sig=True):
        self.wait(*toks)
        if sig:
            self.n += 1
            self.ops.append(lambda e: fn(e).then_inc(self.sem, 1))
        else:
            self.ops.append(fn)
        return (self.sem, self.n)

    def now(self):
        return (self.sem, self.n)

    def play(self, e):
        for op in self.ops:
            op(e)


class Copies:

    def __init__(self, queue, sems):
        self.q, self.sems, self.counts, self.k = queue, sems, [0] * len(sems), 0

    def do(self, out, in_, *toks):
        k = self.k % len(self.sems)
        self.k += 1
        self.q.wait(*toks)
        if self.counts[k]:
            self.q.wait((self.sems[k], self.counts[k]))
        self.counts[k] += 16
        self.q.ops.append(lambda e, s=self.sems[k]: e.dma_start(out, in_).then_inc(s, 16))
        return (self.sems[k], self.counts[k])

    def all(self):
        return [(s, c) for s, c in zip(self.sems, self.counts) if c]


def f(ap):
    return ap.bitcast(F32)


def build(nc, t, NB, stop=None):
    with ExitStack() as ctx:
        sem = lambda n: ctx.enter_context(nc.semaphore(n))
        pe = Queue("pe", sem("s_pe"))
        act = Queue("act", sem("s_act"))
        dve = Queue("dve", sem("s_dve"))
        pool = Queue("pool", sem("s_pool"))
        sp = Queue("sp", sem("s_sp"))
        ld = Copies(sp, [sem(f"s_d{i}") for i in range(48)])
        st = Copies(pool, [sem(f"s_o{i}") for i in range(8)])
        PS = ctx.enter_context(nc.psum_tensor("PS", [P, 8, 512], F32))
        X = ctx.enter_context(nc.sbuf_tensor("X", [P, NB, 4, D], F32))
        ident = ctx.enter_context(nc.sbuf_tensor("ident", [P, P], F32))
        mhalf = ctx.enter_context(nc.sbuf_tensor("mhalf", [P, 16], F32))

        t_id = [ld.do(ident[:], t["c_ident"]),
                pool.do(lambda e: e.memset(mhalf[:], -0.5))]
        xin = []

        def load_x(batches):
            xin.extend(ld.do(X[:, b], t["x"][b].rearrange("(t p) d -> p t d", p=P)) for b in batches)

        load_x([0])

        bank_free = [[] for _ in range(8)]
        tk = {}

        def get(*names):
            return [tk[n] for n in names if n in tk]

        def mm3(out, L, R, first, last, *toks, sig=False):
            pe.wait(*toks)
            pe.do(lambda e: e.matmul(out, L[0], R[0], start=first, stop=False), sig=False)
            pe.do(lambda e: e.matmul(out, L[0], R[1], start=False, stop=False), sig=False)
            return pe.do(lambda e: e.matmul(out, L[1], R[0], start=False, stop=last), sig=sig)

        def layernorm(src, dst, T, toks):
            n = len(src)
            tk = []
            for i in range(n):
                tk.append(dve.do(lambda e, i=i: e.bn_stats(T[:, 6 * i:6 * i + 6], src[i]), *toks))
            ta = []
            for i in range(n):
                ta.append(dve.do(lambda e, i=i: e.bn_aggr(T[:, 32 + 2 * i:34 + 2 * i], T[:, 6 * i:6 * i + 6]), tk[i]))
            var = T[:, 32:32 + 2 * n].rearrange("p (n s) -> p n s", s=2)[:, :, 1]
            r = T[:, 48:48 + n]
            t1 = pool.do(lambda e: e.tensor_scalar(r, var, 1e-5, None, ALU.add), ta[-1])
            t2 = pool.do(lambda e: e.tensor_tensor(r, r, mhalf[:, 0:n], ALU.pow), t1, *t_id)

            def apply(q=dve):
                return [q.do(lambda e, i=i: e.tensor_scalar(
                    dst[i], src[i], T[:, 32 + 2 * i:33 + 2 * i], T[:, 48 + i:49 + i], ALU.subtract, ALU.mult), t2) for i in range(n)][-1]
            return apply

        def names_for(*tensors):
            with ExitStack() as c:
                return [c.enter_context(nc.sbuf_tensor(*a)) for a in tensors]

        with ExitStack() as c1:
            sb = lambda n, s, d: c1.enter_context(nc.sbuf_tensor(n, s, d))
            QS = sb("QS", [P, 2, 16, S], BF16)
            KS = sb("KS", [P, 2, 16, S], BF16)
            HL = sb("HL", [P, 3, 3, S], BF16)
            xT = sb("xT", [P, 2, 2, S], F32R)
            cst = sb("cst", [P, 2, S], F32)
            VP = sb("VP", [P, 2, 4, 16, 17], F32)
            PT = sb("PT", [P, 2, 4, S], F32)
            OT = sb("OT", [P, 2, S], F32)
            OC = sb("OC", [P, 2, S], F32)
            SM = sb("SM", [16, S], F32)
            OCr = sb("OCr", [P, 2, 2, S], F32R)
            TM = sb("TM", [P, 2, S], F32)
            MX = sb("MX", [P, 2, 4, 16], F32)
            MB = sb("MB", [P, 2, 4, 3, 8], BF16)
            MR = sb("MR", [P, 4, 8], F32)
            identb = sb("identb", [P, P], BF16)
            NM = sb("NM", [24, S], BF16)
            W0, WO0 = names_for(("W0", [P, 2, 2, 5, D], F32), ("WO0", [P, 2, 2, 2, D], F32))
            W = sb("W", [P, 2, 2, 5, D], F32R)
            WO = sb("WO", [P, 2, 2, 2, D], F32R)
            LNT = sb("LNT", [P, 2, 64], F32)
            tab = sb("tab", [P, 2, S], F32)
            RCX = sb("RCX", [P, 64, 16], F32)
            RCT = sb("RCT", [P, 64], F32)
            bq = sb("bq", [P, 4], F32)
            bb = sb("bb", [P, 2, D], F32)

            t_ones = []
            t_idb = dve.do(lambda e: e.tensor_copy(identb[:], ident[:]), *t_id)
            t_ones.append(pool.do(lambda e: e.memset(VP[:], 1.0)))
            bank_free[6] = [dve.do(lambda e: e.memset(PS[:, 6, :], 0.0))]

            def load_weights(kind, free):
                x = int(kind == "x")
                jobs = []
                for j, name in enumerate("qkvo"):
                    for kc in range(2):
                        if j < 3:
                            raw, h, l = W0[:, kc, 1, j], W[:, kc, 0, j], W[:, kc, 1, j]
                        else:
                            raw, h, l = WO0[:, x, kc, 1], WO[:, x, kc, 0], WO[:, x, kc, 1]
                        jobs.append((j, kc, raw, h, l, ld.do(raw, t[f"{kind}_{name}"][kc * P:(kc + 1) * P, :], free)))
                for j, kc, raw, h, l, a in jobs:
                    b = act.do(lambda e, h=h, raw=raw: e.copy(h, raw), a)
                    c = [dve.do(lambda e, h=h, l=l, raw=raw: e.tensor_tensor(l, raw, f(h), ALU.subtract), b)]
                    if kind == "s" and j < 2:
                        for hl in range(2):
                            s2 = W[:, kc, hl, j].rearrange("p (n two) -> p n two", two=2)
                            d2 = W[:, kc, hl, 3 + j].rearrange("p (n two) -> p n two", two=2)
                            c.append(pool.do(lambda e, s2=s2, d2=d2: e.tensor_scalar(
                                d2[:, :, 0], f(s2[:, :, 1]), -1.0, None, ALU.mult), c[0]))
                            c.append(pool.do(lambda e, s2=s2, d2=d2: e.tensor_copy(
                                d2[:, :, 1], f(s2[:, :, 0])), c[0]))
                    tk.setdefault(("W", x, j), []).extend(c)

            NV = NB if stop == "self" else 0 if stop and stop[0] == "f" else 2 * NB

            def misc(fn_pe, readers):
                pe.wait(bank_free[7])
                m = fn_pe()
                bank_free[7] = readers(m)

            def chunk_transposes(vb):
                b, cross = vb % NB, vb >= NB

                def one(half):
                    def go():
                        w = get(("X", vb)) if cross else [xin[b]]

                        def mms():
                            pe.wait(w, t_id)
                            for i in range(4):
                                r = pe.do(lambda e, i=i: e.transpose(PS[:, 7, i * P:(i + 1) * P],
                                                                     X[:, b, i, half * P:(half + 1) * P], ident[:]),
                                          sig=(i == 3))
                            return r

                        def rd(m):
                            a = act.do(lambda e: e.copy(xT[:, half, 0], PS[:, 7, :]), m, get(("xTfree",)))
                            d = dve.do(lambda e: e.tensor_tensor(xT[:, half, 1], PS[:, 7, :], f(xT[:, half, 0]), ALU.subtract), a)
                            tk[("xT", vb, half)] = [a, d]
                            return [a, d]
                        misc(mms, rd)
                    return go

                def load():
                    tk["ctx", b] = ld.do(cst[:], t["ctxT"][:, b * S:(b + 1) * S].rearrange("(k p) s -> p k s", p=P), get(("cstfree",)))

                def ctxt():
                    a = tk["ctx", b]
                    free = [pe.now()]
                    r = []
                    for kc in range(2):
                        h = act.do(lambda e, kc=kc: e.copy(xT[:, kc, 0], cst[:, kc]), a, free)
                        r.append(h)
                        r.append(dve.do(lambda e, kc=kc: e.tensor_tensor(xT[:, kc, 1], cst[:, kc], f(xT[:, kc, 0]), ALU.subtract), h, a, free))
                    tk[("cstfree",)] = list(r)
                    tk[("xT", vb, 0)] = tk[("xT", vb, 1)] = r
                return [one(0), one(1)], ctxt, load

            def act_in(vb):
                return get(("xT", vb, 0), ("xT", vb, 1))

            later = []

            def split3(x, parts, r, ready, free, done):
                a = act.do(lambda e: e.copy(parts[0], x), ready, free)
                b = pool.do(lambda e: e.tensor_tensor(r, x, parts[0], ALU.subtract), a, ready, get(("rfree",)))

                def rest():
                    c = act.do(lambda e: e.copy(parts[1], r), b)
                    d = pool.do(lambda e: e.tensor_tensor(parts[2], r, parts[1], ALU.subtract), c, b)
                    tk[("rfree",)] = [d]
                    tk[("TMfree",)] = [a, b, c, d]
                    done([a, c, d])
                later.append(rest)

            def to_dram(vb, qk, tile, ready):
                hb = 2 if qk else tile
                tk["HS", vb, qk, tile] = w = ld.do(t["hs"][vb % 2, 2 * qk + tile], HL[:, hb], ready, get(("HSfree", vb % 2, qk, tile)))
                tk["HLfree", hb] = [w]

            def chunk_qk(vb, qk, tile):
                cross = vb >= NB

                def wt(j, kc, cols):
                    return (W[:, kc, 0, j, cols], W[:, kc, 1, j, cols])
                cols = slice(tile * P, (tile + 1) * P)

                def gemm(j):
                    def mms():
                        pe.wait(act_in(vb), tk["W", int(cross), qk])
                        for kc in range(2):
                            r = mm3(PS[:, 7, :], wt(j, kc, cols), (xT[:, kc, 0], xT[:, kc, 1]), kc == 0, kc == 1, sig=kc == 1)
                        return r
                    return mms
                hb = 2 if qk else tile
                parts = [HL[:, hb, k] for k in range(3)]

                if cross:
                    def go():
                        def rd(m):
                            bias = bq[:, 2 * qk + tile:2 * qk + tile + 1]
                            a = act.do(lambda e: e.activation(TM[:, 0], PS[:, 7, :], ACT.Identity, bias=bias), m, get(("TMfree",)), t_bq)
                            split3(TM[:, 0], parts, TM[:, 1], a, get(("HLfree", hb)), lambda r: to_dram(vb, qk, tile, r))
                            return [a]
                        misc(gemm(qk), rd)
                    return [go]

                def go1():
                    def rd(m):
                        d = dve.do(lambda e: e.scalar_tensor_tensor(out=TM[:, 0], in0=PS[:, 7, :], scalar=1.0 if qk else 0.25, in1=tab[:, 0],
                                                                    op0=ALU.mult, op1=ALU.mult), m, t_tab, get(("TMfree",)))
                        tk["t1"] = d
                        return [d]
                    misc(gemm(qk), rd)

                def go2():
                    def rd(m):
                        d = dve.do(lambda e: e.scalar_tensor_tensor(out=TM[:, 1], in0=PS[:, 7, :], scalar=1.0 if qk else 0.25, in1=tab[:, 1],
                                                                    op0=ALU.mult, op1=ALU.mult), m, get(("TMfree",)))
                        x = pool.do(lambda e: e.tensor_tensor(TM[:, 0], TM[:, 0], TM[:, 1], ALU.add), d, tk["t1"])
                        split3(TM[:, 0], parts, TM[:, 1], x, get(("HLfree", hb)), lambda r: to_dram(vb, qk, tile, r))
                        return [d]
                    misc(gemm(3 + qk), rd)
                return [go1, go2]

            def chunk_v(vb, half):
                cross = vb >= NB

                def go():
                    def mms():
                        pe.wait(act_in(vb), tk["W", int(cross), 2])
                        for i in range(2):
                            tt = 2 * half + i
                            tok = slice(tt * P, (tt + 1) * P)
                            for kc in range(2):
                                r = mm3(PS[:, 7, i * D:(i + 1) * D], (xT[:, kc, 0, tok], xT[:, kc, 1, tok]),
                                        (W[:, kc, 0, 2], W[:, kc, 1, 2]), kc == 0, kc == 1, sig=kc == 1)
                        return r

                    def rd(m):
                        src = PS[:, 7, :].rearrange("p (t h d) -> p t h d", t=2, d=16)
                        dst = VP[:, vb % 2, 2 * half:2 * half + 2, :, 0:16]
                        free = get(("VPfree", vb % 2))
                        if cross:
                            r = []
                            for i in range(2):
                                r.append(dve.do(lambda e, i=i: e.tensor_tensor(
                                    dst[:, i], src[:, i], bb[:, 0].rearrange("p (h d) -> p h d", d=16), ALU.add),
                                    m, free, t_bb, t_ones))
                        else:
                            r = [act.do(lambda e, i=i: e.copy(dst[:, i], src[:, i]), m, free, t_ones) for i in range(2)]
                        tk["V", vb, half] = r
                        return r
                    misc(mms, rd)
                return go

            def stack(vb, tile):
                s = vb % 2
                free = get(("Bdone", vb - 2, 2 * tile + 1), ("Adone", vb - 2, 2 * tile + 1))
                r = []
                for qk, T, blocks in ((0, QS, (0, 0, 0, 1, 1, 2)), (1, KS, (0, 1, 2, 0, 1, 0))):
                    hs = t["hs"][s, 2 * qk + tile]
                    w = tk["HS", vb, qk, tile]
                    v = hs.rearrange("(h d) a t -> a d h t", d=16)
                    rr = [ld.do(T[16 * k:16 * k + 16, s, 8 * tile:8 * tile + 8], v[a], w, free) for k, a in enumerate(blocks)]
                    tk["HSfree", s, qk, tile] = rr
                    r += rr
                for g in (2 * tile, 2 * tile + 1):
                    tk["ST", vb, g] = r

            def a_pass(vb, g, qt, p):
                s = vb % 2
                for par in range(2):
                    h = 4 * g + 2 * p + par
                    slot = 4 + par
                    pe.wait(bank_free[slot], tk["ST", vb, g])
                    m = pe.do(lambda e, h=h, slot=slot: e.matmul(
                        PS[:, slot, :], QS[0:96, s, h, qt * P:(qt + 1) * P], KS[0:96, s, h, :],
                        start=True, stop=True))
                    d = dve.do(lambda e, h=h, slot=slot: e.tensor_reduce(
                        MX[:, s, qt, h:h + 1], PS[:, slot, :], AX, ALU.max), m, get(("MXfree", vb - 2, g)))
                    bank_free[slot] = [d]
                    tk["MX", vb, g] = d
                    tk[("Adone", vb, g)] = m

            def max_rows(vb, half):
                s = vb % 2
                src = MX[:, s, :, 8 * half:8 * half + 8]
                part = [MB[:, half, :, k] for k in range(3)]
                a = dve.do(lambda e: e.tensor_copy(part[0], src), tk["MX", vb, 2 * half], tk["MX", vb, 2 * half + 1], get(("MBfree", half)))
                b = dve.do(lambda e: e.tensor_tensor(MR[:], src, part[0], ALU.subtract), a)
                c = dve.do(lambda e: e.tensor_copy(part[1], MR[:]), b)
                d = dve.do(lambda e: e.tensor_tensor(part[2], MR[:], part[1], ALU.subtract), c)
                tk[("MXfree", vb, 2 * half)] = tk[("MXfree", vb, 2 * half + 1)] = b
                tk["MB", vb, half] = d

            def max_transposes(vb, half):
                s = vb % 2
                out = PS[:, 7, :].bitcast(BF16)

                def mms():
                    pe.wait(tk["MB", vb, half], t_idb)
                    for qt in range(4):
                        r = pe.do(lambda e, qt=qt: e.transpose(
                            out[0:24, qt * P:(qt + 1) * P], MB[:, half, qt].rearrange("p a h -> p (a h)"),
                            identb[:]), sig=qt == 3)
                    return r

                def rd(m):
                    tk[("MBfree", half)] = [m]
                    n = act.do(lambda e: e.activation(NM[:], out[0:24, 0:S], ACT.Copy, scale=-1.0), m, get(("NMfree",)))
                    r = ld.do(QS[96:99, s, 8 * half:8 * half + 8], NM[:], n, get(("Bdone", vb - 2, 2 * half + 1)))
                    tk[("NMfree",)] = [r]
                    tk["NR", vb, 2 * half] = tk["NR", vb, 2 * half + 1] = [r]
                    return [n]
                misc(mms, rd)

            def b_scores(vb, g, kt, p):
                s = vb % 2
                buf = kt % 2
                pe.wait(bank_free[2 * p], tk["NR", vb, g], t_ones)
                for par in range(2):
                    h = 4 * g + 2 * p + par
                    m = pe.do(lambda e, h=h, par=par: e.matmul(
                        PS[:, 2 * p + par, :], KS[0:99, s, h, kt * P:(kt + 1) * P], QS[0:99, s, h, :],
                        start=True, stop=True), sig=par == 1)
                tk[("Bdone", vb, g)] = m
                a = act.do(lambda e: e.activation(PT[:, buf, 2 * p:2 * p + 2], PS[:, 2 * p:2 * p + 2, :], ACT.Exp),
                           m, get(("PTfree", buf)))
                bank_free[2 * p] = [a]
                tk["PT", buf] = a

            def pv(vb, g, kt):
                s = vb % 2
                buf = kt % 2
                pe.wait(tk["PT", buf], tk["V", vb, 0], tk["V", vb, 1])
                if kt == 0:
                    pe.wait(bank_free[6])
                for hh in range(4):
                    m = pe.do(lambda e, hh=hh: e.matmul(
                        PS[32 * hh:32 * hh + 17, 6, :], VP[:, s, kt, 4 * g + hh, :], PT[:, buf, hh, :],
                        start=kt == 0, stop=kt == 3), sig=hh == 3)
                tk[("PTfree", buf)] = [m]
                if g == 3:
                    tk[("VPfree", s)] = [m]
                if kt == 3:
                    o = g % 2
                    a = act.do(lambda e: e.copy(OT[:, o], PS[:, 6, :]), m, get(("OTfree", o)))
                    bank_free[6] = [a]
                    r = []
                    for hh in range(4):
                        h = 4 * g + hh
                        r.append(ld.do(OC[16 * (h % 8):16 * (h % 8) + 16, h // 8], OT[32 * hh:32 * hh + 16, o], a, get(("OCfree", h // 8))))
                    r.append(ld.do(SM[4 * g:4 * g + 4], OT[16:P:32, o], a, get(("SMfree",))))
                    tk[("OTfree", o)] = r
                    tk.setdefault(("OC", vb), []).extend(r)

            def bias_out(vb):
                tk["XB", vb] = [pool.do(lambda e, i=i: e.tensor_tensor(X[:, vb % NB, i], X[:, vb % NB, i], bb[:, 1], ALU.add),
                                        [pe.now()], t_bb) for i in range(4)]

            def chunk_out(vb):
                b, cross = vb % NB, vb >= NB

                def inverse():
                    def mms():
                        pe.wait(tk["OC", vb], t_id)
                        for i in range(4):
                            m = pe.do(lambda e, i=i: e.transpose(PS[:, 7, 16 * i:16 * i + 16], SM[:, i * P:(i + 1) * P],
                                                                 ident[0:16, 0:16]), sig=i == 3)
                        tk[("SMfree",)] = [m]
                        return m

                    def rd(m):
                        d = dve.do(lambda e: e.reciprocal(RCT[:], PS[:, 7, 0:64]), m, get(("rc",)))
                        tk["rc"] = tk[("rc",)] = act.do(lambda e: e.copy(RCX[:], RCT[:].unsqueeze(2).broadcast_to([P, 64, 16])),
                                                         d, get(("RCXfree",)))
                        return [d]
                    misc(mms, rd)

                def norm(tile):
                    def go():

                        def mms():
                            pe.wait(tk["rc"])
                            for i in range(4):
                                m = pe.do(lambda e, i=i: e.transpose(
                                    PS[:, 7, i * P:(i + 1) * P],
                                    RCX[:, 16 * i + 8 * tile:16 * i + 8 * tile + 8].rearrange("p h d -> p (h d)"),
                                    ident[:]), sig=i == 3)
                            tk[("RCXfree",)] = [m]
                            return m

                        def rd(m):
                            free = get(("OCrfree",))
                            d = dve.do(lambda e: e.tensor_tensor(OC[:, tile], OC[:, tile], PS[:, 7, :], ALU.mult), m, tk["OC", vb])
                            a = act.do(lambda e: e.copy(OCr[:, tile, 0], OC[:, tile]), d, free)
                            l = pool.do(lambda e: e.tensor_tensor(OCr[:, tile, 1], OC[:, tile], f(OCr[:, tile, 0]), ALU.subtract), a, d, free)
                            tk["OCr", vb, tile] = [a, l]
                            tk[("OCfree", tile)] = [l, a]
                            return [d]
                        misc(mms, rd)
                    return go

                def proj(half):
                    def go():
                        def mms():
                            pe.wait(tk["OCr", vb, 0], tk["OCr", vb, 1], tk["W", int(cross), 3])
                            for i in range(2):
                                tok = slice((2 * half + i) * P, (2 * half + i + 1) * P)
                                for kc in range(2):
                                    r = mm3(PS[:, 7, i * D:(i + 1) * D], (OCr[:, kc, 0, tok], OCr[:, kc, 1, tok]),
                                            (WO[:, int(cross), kc, 0], WO[:, int(cross), kc, 1]), kc == 0, kc == 1, sig=kc == 1)
                            return r

                        def rd(m):
                            if half == 1:
                                tk[("OCrfree",)] = [m]
                            xx = X[:, b, 2 * half:2 * half + 2]
                            d = dve.do(lambda e: e.tensor_tensor(xx, PS[:, 7, :].rearrange("p (t d) -> p t d", t=2), xx, ALU.add),
                                       m, get(("XB", vb)))
                            w = [d]
                            tiles = [X[:, b, 2 * half + i] for i in range(2)]
                            tk["LN", vb, half] = layernorm(tiles, tiles, LNT[:, half], w)
                            return [d]
                        misc(mms, rd)
                    return go

                def apply(half):
                    def go():
                        l = tk["LN", vb, half](pool)
                        tk.setdefault(("X", vb + NB), []).append(l)
                        if cross:
                            st.do(t["x2s"][b, :, 2 * half:2 * half + 2, :], X[:, b, 2 * half:2 * half + 2], l)
                    return go
                return [inverse, norm(0), norm(1), proj(0), apply(0), proj(1), apply(1)]

            load_weights("s", [])
            t_tab = ld.do(tab[:], t["c_tab"])
            t_bq = ld.do(bq[:], t["xbqk"])
            t_bb = ld.do(bb[:], t["xbvo"])
            load_x(range(1, NB))

            def place(chunks):
                now = later[:]
                later.clear()
                for c in now + chunks:
                    c()

            for step in range(-1, NV + 2):
                vbA, vbB, vbP, vbO = step, step - 1, step + 1, step - 2
                hasA, hasB, hasP, hasO = 0 <= vbA < NV, 0 <= vbB < NV, vbP < NV, 0 <= vbO < NV
                at = [[] for _ in range(33)]
                if hasB:
                    at[0].append(lambda: max_transposes(vbB, 1))
                if hasA:
                    at[1].append(chunk_v(vbA, 0))
                    at[3] += [chunk_v(vbA, 1), lambda: tk.__setitem__(("xTfree",), [pe.now()])]
                    at[16].append(lambda: max_rows(vbA, 0))
                    at[18].append(lambda: max_transposes(vbA, 0))
                    at[32].append(lambda: max_rows(vbA, 1))
                if hasP and vbP == NB:
                    at[3].append(lambda: load_weights("x", [pe.now()]))
                if hasO:
                    for i, c in zip((2, 5, 7, 11, 13, 15, 17), chunk_out(vbO)):
                        at[i].append(c)
                if step == -1:
                    for i in range(4):
                        at[18 + 4 * i].append(lambda i=i: t_ones.append(dve.do(
                            lambda e: e.memset(KS[96:P, i // 2, 8 * (i % 2):8 * (i % 2) + 8], 1.0))))
                if hasP:
                    tr, ctxt, load = chunk_transposes(vbP)
                    if vbP >= NB:
                        at[5].append(load)
                    at[4].append(tr[0])
                    at[6].append(tr[1])
                    q0, q1, k0, k1 = (chunk_qk(vbP, qk, tile) for qk in (0, 1) for tile in (0, 1))
                    order = q0 + q1 + [ctxt] + k0 + k1 if vbP >= NB else q0 + k0 + q1 + k1
                    for i, c in zip((8, 10, 12, 16, 22) if vbP >= NB else (8, 10, 12, 14, 20, 21, 24, 25), order):
                        at[i].append(c)
                    at[17].append(lambda: stack(vbP, 0))
                    if vbP >= NB:
                        at[18].append(lambda: bias_out(vbP))
                    at[32].append(lambda: stack(vbP, 1))
                for g in range(4):
                    for k in range(4):
                        i = 8 * g + 2 * k
                        if hasB:
                            b_scores(vbB, g, k, 0)
                        if hasA:
                            a_pass(vbA, g, k, 0)
                        place(at[i])
                        if hasB:
                            b_scores(vbB, g, k, 1)
                        if hasA:
                            a_pass(vbA, g, k, 1)
                        place(at[i + 1])
                        if hasB and (k or g):
                            pv(vbB, g if k else g - 1, (k - 1) % 4)
                if hasB:
                    pv(vbB, 3, 3)
                place(at[32])
                if stop in ("att", "self") and step == NV + 1:
                    for b in range(NB):
                        st.do(t["out"][b].rearrange("(t p) d -> p t d", p=P), X[:, b], tk[("X", NV + b)])
        if stop not in ("att", "self"):
            for b in range(NB):
                if NV:
                    tk["FX", 0, b] = tk["X", 2 * NB + b]
                else:
                    tk["FX", 0, b] = [xin[b]]
                    st.do(t["x2s"][b], X[:, b], xin[b])
            ffn(nc, ctx, t, NB, stop, dict(pe=pe, act=act, dve=dve, pool=pool, sp=sp, ld=ld, st=st, PS=PS, X=X,
                                           ident=ident, mhalf=mhalf, t_id=t_id, tk=tk, mm3=mm3, get=get,
                                           layernorm=layernorm, names_for=names_for))
        queues_end(nc, ctx, pe, act, dve, pool, sp, ld, st)


def ffn(nc, ctx, t, NB, stop, g):
    pe, act, dve, pool, sp, ld, st = (g[n] for n in ("pe", "act", "dve", "pool", "sp", "ld", "st"))
    PS, X, ident, mhalf, t_id, tk, mm3, get, layernorm, names_for = (g[n] for n in (
        "PS", "X", "ident", "mhalf", "t_id", "tk", "mm3", "get", "layernorm", "names_for"))
    engines = (pe, act, dve, pool, sp)
    free = [[] for _ in range(8)]

    def barrier():
        all_ = [q.now() for q in (pe, act, dve, pool)] + ld.all() + st.all()
        for q in engines:
            q.wait(all_)

    barrier()
    sb = lambda n, s, d: ctx.enter_context(nc.sbuf_tensor(n, s, d))

    WQ0, WOF0, W10, W20 = names_for(("WQ0", [P, 2, 2, 1536], F32), ("WOF0", [P, 4, 2, D], F32),
                                    ("W10", [P, 2, 2, 1408], F32), ("W20", [P, 6, 2, D], F32))
    WQ = sb("WQ", [P, 2, 2, 1536], F32R)
    WOF = sb("WOF", [P, 4, 2, D], F32R)
    W1 = sb("W1", [P, 2, 2, 1408], F32R)
    W2 = sb("W2", [P, 6, 2, D], F32R)
    rot = sb("rot", [P, 4, 4, 64], F32)
    mask = sb("mask", [P, 2, 256], BF16)
    identb = sb("identbf", [P, P], BF16)
    cols = sb("cols", [P, 2, 16], F32)
    b2 = sb("b2", [P, 2, D], F32)
    XS, HN, ST = names_for(("XS", [P, 2, 4, P], F32), ("HN", [P, 2, 4, D], F32), ("ST", [P, 2, 128], F32))
    XT = sb("XT", [P, 2, 2, 2, S + 2], F32R)
    xt_free = [[]]
    qks = sb("qks", [P, 2, 4, 64], F32)
    mk = sb("mk", [P, 256], F32)
    t_mk = ld.do(mk[:], t["c_mask"])
    t_qks = ld.do(qks[:], t["f_qks"])

    def rotations(L, ready):
        a = ld.do(rot[:], t["c_rot"], ready)
        return [dve.do(lambda e, j=j: e.tensor_tensor(
            rot[:, j], rot[:, j], qks[:, L, j:j + 1, :].broadcast_to([P, 4, 64]), ALU.mult), a, t_qks) for j in range(4)]

    tk["rot", 0] = rotations(0, [])
    t_mask = [dve.do(lambda e, i=i: e.tensor_copy(mask[:, i], mk[:]), t_mk) for i in range(2)]
    t_cols = [ld.do(cols[:], t["f_cols"]), ld.do(b2[:], t["f_b2"])]
    t_mask.append(dve.do(lambda e: e.tensor_copy(identb[:], ident[:])))

    def weights(pairs, ready, key, low):
        tk[key] = []
        out = []
        for hi, lo, raw, src in pairs:
            a = ld.do(raw, src, ready)

            def split(hi=hi, lo=lo, raw=raw, a=a):
                h = act.do(lambda e: e.copy(hi, raw), a)
                tk[key].append(low.do(lambda e: e.tensor_tensor(lo, raw, f(hi), ALU.subtract), h))
            out.append(split)
        return out

    def load_attn(L, ready, low):
        pairs = []
        for c in range(3):
            for kc in range(2):
                n = slice(512 * c, 512 * c + 512)
                pairs.append((WQ[:, kc, 0, n], WQ[:, kc, 1, n], WQ0[:, kc, 1, n], t["f_wqkv"][L, kc * P:(kc + 1) * P, n]))
        for kc in range(4):
            pairs.append((WOF[:, kc, 0], WOF[:, kc, 1], WOF0[:, kc, 1], t["f_wo"][L, kc * P:(kc + 1) * P, :]))
        return weights(pairs, ready, ("WA", L), low)

    def load_mlp(L, ready, low):
        pairs = []
        for kc in range(2):
            for c in range(2):
                n = slice(704 * c, 704 * c + 704)
                pairs.append((W1[:, kc, 0, n], W1[:, kc, 1, n], W10[:, kc, 1, n], t["f_w1"][L, kc * P:(kc + 1) * P, n]))
        for kc in range(6):
            pairs.append((W2[:, kc, 0], W2[:, kc, 1], W20[:, kc, 1], t["f_w2"][L, kc * P:(kc + 1) * P, :]))
        return weights(pairs, ready, ("WM", L), low)

    def xtokens(L, b):
        return get(("FX", L, b))

    def attention_start(L):
        loc = {}
        t_z = [dve.do(lambda e: e.memset(f(XT[:, :, 1, :, 0:1]), 0.0), xt_free[0])]

        def lg(*names):
            return [loc[n] for n in names if n in loc]

        def misc(mms, rd, bank=2):
            pe.wait(free[bank])
            free[bank] = rd(mms())

        def xt(b, half):
            bp = b % 2

            def mms():
                pe.wait(xtokens(L, b), t_id)
                for i in range(4):
                    r = pe.do(lambda e, i=i: e.transpose(PS[:, 2, i * P:(i + 1) * P], X[:, b, i, half * P:(half + 1) * P],
                                                         ident[:]), sig=i == 3)
                return r

            def rd(m):
                h, l = (XT[:, bp, half, k, half:half + S] for k in range(2))
                w = [lg(("XTread", b - 2)), xt_free[0]]
                a = act.do(lambda e: e.copy(h, PS[:, 2, :]), m, w)
                d = dve.do(lambda e: e.tensor_tensor(l, PS[:, 2, :], f(h), ALU.subtract), a, m, w)
                loc["XT", b, half] = [a, d]
                return [a, d]
            misc(mms, rd)

        for h in range(2):
            xt(0, h)
        return loc, lg, misc, xt, t_z

    def attention(L, start, chores, ahead):
        with ExitStack() as c2:
            s2 = lambda n, s, d: c2.enter_context(nc.sbuf_tensor(f"{n}{L}", s, d))
            qT = s2("qT", [P, 2, 4, 2, P], F32R)
            kT = s2("kT", [P, 4, 2, S], F32R)
            V = s2("V", [P, 4, S], F32)
            SQ = s2("SQ", [P, 2, S], F32)
            RA = s2("RA", [P, 2, S], F32)
            RB = s2("RB", [P, 2, S], F32)
            RI = s2("RI", [P, 2, 8], F32)
            PB = s2("PB", [P, 2, 8, 256], F32)
            PTB = s2("PTB", [P, 4, 4, P], F32)
            NM = s2("NMf", [P, 2, 8], F32)
            SUM = s2("SUM", [P, 2, 8], F32)
            RC = s2("RC", [P, 8], F32)
            O = s2("O", [P, S], F32)
            OTr = s2("OTr", [P, 2, 4, P], F32R)
            loc, lg, misc, xt, t_z = start
            t_rot = tk["rot", L]

            def gemm(u, part, bank):
                b, i = divmod(u, 4)
                pe.wait(loc["XT", b, 0], loc["XT", b, 1], t_z, tk["WA", L][2 * part:2 * part + 2], free[bank])
                for kc in range(2):
                    r = mm3(PS[:, bank, :], [XT[:, b % 2, kc, k, i * P:(i + 1) * P] for k in range(2)],
                            [WQ[:, kc, k, part * S:(part + 1) * S] for k in range(2)], kc == 0, kc == 1, sig=kc == 1)
                if part == 2 and i == 3:
                    loc["XTread", b] = r
                return r

            def qk_post(u, part, bank, m):
                i = u % 4
                ps = PS[:, bank, :]
                psh = ps.rearrange("p (h d) -> p h d", d=64)
                w = lg(("Rfree", part))
                a0 = act.do(lambda e: e.activation(SQ[:, part], ps, ACT.Square), m, lg(("SQfree", part)))
                d1 = dve.do(lambda e: e.tensor_tensor(RA[:, part].rearrange("p (h d) -> p h d", d=64), psh,
                                                      rot[:, 2 * part, i:i + 1, :].broadcast_to([P, 8, 64]), ALU.mult), a0, w, t_rot)
                rb = RB[:, part].rearrange("p (h d) -> p h d", d=64)
                d2 = [dve.do(lambda e, o=o: e.tensor_tensor(
                    rb[:, :, o:o + 32], psh[:, :, 32 - o:64 - o],
                    rot[:, 2 * part + 1, i:i + 1, o:o + 32].broadcast_to([P, 8, 32]), ALU.mult), a0, w, t_rot) for o in (0, 32)]
                free[bank] = [a0, d1] + d2
                loc["qk", part] = (a0, d1, d2)

            def qk_post2(u, part):
                a0, d1, d2 = loc["qk", part]
                d3 = dve.do(lambda e: e.tensor_reduce(RI[:, part], SQ[:, part].rearrange("p (h d) -> p h d", d=64), AX, ALU.add),
                            a0, lg(("RIfree", part)))
                loc["SQfree", part] = [d3]
                p1 = pool.do(lambda e: e.tensor_scalar(RI[:, part], RI[:, part], 1e-24, None, ALU.max), d3)
                p2 = pool.do(lambda e: e.tensor_tensor(RI[:, part], RI[:, part], mhalf[:, 0:8], ALU.pow), p1)
                p3 = dve.do(lambda e: e.tensor_tensor(RA[:, part], RA[:, part], RB[:, part], ALU.add), d1, d2)
                ra = RA[:, part].rearrange("p (h d) -> p h d", d=64)
                p4 = pool.do(lambda e: e.tensor_tensor(ra, ra, RI[:, part].unsqueeze(2).broadcast_to([P, 8, 64]), ALU.mult), p3, p2)
                loc["RIfree", part] = [p4]
                loc["R", u, part] = [p4]

            def qkt(u, part):
                b, i = divmod(u, 4)

                def mms():
                    pe.wait(loc["R", u, part])
                    for c in range(4):
                        r = pe.do(lambda e, c=c: e.transpose(PS[:, 2 - part, c * P:(c + 1) * P], RA[:, part, c * P:(c + 1) * P], ident[:]),
                                  sig=c == 3)
                    loc["Rfree", part] = [r]
                    return r

                def rd(m):
                    src = PS[:, 2 - part, :].rearrange("p (c t) -> p c t", t=P)
                    if part == 0:
                        h, l = (qT[:, u % 2, :, k] for k in range(2))
                        w = lg(("Sdone", u - 2))
                    else:
                        h, l = (kT[:, :, k, i * P:(i + 1) * P] for k in range(2))
                        w = lg(("Sdone", u - 3))
                    a = act.do(lambda e: e.copy(h, src), m, w)
                    d = dve.do(lambda e: e.tensor_tensor(l, src, f(h), ALU.subtract), a, m, w)
                    loc["T", u, part] = [a, d]
                    return [a, d]
                misc(mms, rd, 2 - part)

            def heads(hp):
                h = 4 * (hp // 2) + hp % 2
                return (h, h + 2)

            def scores(u, hp):
                b, i = divmod(u, 4)
                bank = 4 + hp % 2
                k0 = 0 if i else P
                pe.wait(free[bank], t_mask, loc["T", u, 0], loc["T", u, 1])
                out = PS[:, bank, :].rearrange("p (h k) -> p h k", h=2)
                pe.do(lambda e: e.matmul(out[:, :, k0:], identb[:], mask[:, :, k0:], start=True, stop=False,
                                         skip_group_check=True), sig=False)
                keys = slice((i - 1) * P if i else 0, (i + 1) * P)
                for x, y in ((0, 0), (0, 1), (1, 0)):
                    for h in range(2):
                        hh = heads(hp)[h]
                        rows = slice(64 * (hh % 2), 64 * (hh % 2) + 64)
                        m = pe.do(lambda e, h=h, hh=hh, rows=rows, x=x, y=y: e.matmul(
                            out[:, h, k0:], qT[rows, u % 2, hh // 2, x], kT[rows, hh // 2, y, keys], start=False, stop=x == 1,
                            skip_group_check=True), sig=h == 1 and x == 1)
                if hp == 3:
                    loc["Sdone", u] = [m]
                d = dve.do(lambda e: e.tensor_reduce(NM[:, u % 2, heads(hp)[0]:heads(hp)[1] + 1:2], out[:, :, k0:], AX, ALU.max, negate=True),
                           m, lg(("E", u - 2)))
                ex = []
                for h in range(2):
                    hh = heads(hp)[h]
                    ex.append(act.do(lambda e, h=h, hh=hh: e.activation(
                        PB[:, u % 2, hh, k0:], out[:, h, k0:], ACT.Exp, bias=NM[:, u % 2, hh:hh + 1],
                        accum_out=SUM[:, u % 2, hh:hh + 1]), d, m, lg(("PBfree", u - 2), ("SUMfree", u - 2))))
                free[bank] = ex
                loc["E", u] = loc["E", u, hp] = ex

            def ptrans(u, hp):
                i = u % 4
                bank = 6 + hp % 2
                pe.wait(free[bank], loc["E", u, hp])
                js = (0, 1) if i else (1,)
                for h in range(2):
                    for j in js:
                        m = pe.do(lambda e, h=h, j=j: e.transpose(
                            PS[:, bank, (2 * h + j) * P:(2 * h + j + 1) * P],
                            PB[:, u % 2, heads(hp)[h], j * P:(j + 1) * P], ident[:]), sig=h == 1 and j == 1)
                src = PS[:, bank, :].rearrange("p (h j q) -> p h j q", h=2, j=2)
                dst = PTB[:, hp].rearrange("p (h j) q -> p h j q", h=2)
                if i == 0:
                    src, dst = src[:, :, 1], dst[:, :, 1]
                w = lg(("PV", u - 1, hp))
                a = act.do(lambda e: e.copy(dst, src), m, w)
                free[bank] = [a]
                loc["PT", u, hp] = [a]
                if hp == 3:
                    loc["PBfree", u] = [m]

            def pv(u, hp):
                b, i = divmod(u, 4)
                pe.wait(loc["PT", u, hp], loc["V", u])
                if hp == 0:
                    pe.wait(free[3])
                js = (0, 1) if i else (1,)
                for h in range(2):
                    hh = heads(hp)[h]
                    for j in js:
                        m = pe.do(lambda e, h=h, j=j, hh=hh: e.matmul(
                            PS[:, 3, hh * 64:hh * 64 + 64], PTB[:, hp, 2 * h + j], V[:, i - 1 + j, hh * 64:hh * 64 + 64],
                            start=j == js[0], stop=j == 1), sig=h == 1 and j == 1)
                loc["PV", u, hp] = [m]
                if hp == 2:
                    loc["SUMfree", u] = [dve.do(lambda e: e.reciprocal(RC[:], SUM[:, u % 2]), loc["E", u], lg(("O", u - 1)))]
                if hp == 3:
                    loc["Vfree", u] = [m]
                    r = loc["SUMfree", u]
                    d = dve.do(lambda e: e.tensor_tensor(
                        O[:].rearrange("p (h d) -> p h d", d=64), PS[:, 3, :].rearrange("p (h d) -> p h d", d=64),
                        RC[:].unsqueeze(2).broadcast_to([P, 8, 64]), ALU.mult), m, r, lg(("Oread",)))
                    free[3] = [d]
                    loc["O", u] = [d]

            def ot(u):
                def mms():
                    pe.wait(loc["O", u])
                    for c in range(4):
                        r = pe.do(lambda e, c=c: e.transpose(PS[:, 2, c * P:(c + 1) * P], O[:, c * P:(c + 1) * P], ident[:]),
                                  sig=c == 3)
                    loc[("Oread",)] = [r]
                    return r

                def rd(m):
                    src = PS[:, 2, :].rearrange("p (c t) -> p c t", t=P)
                    w = lg(("OTfree",))
                    a = act.do(lambda e: e.copy(OTr[:, 0], src), m, w)
                    d = dve.do(lambda e: e.tensor_tensor(OTr[:, 1], src, f(OTr[:, 0]), ALU.subtract), a, m, w)
                    loc["OT", u] = [a, d]
                    return [a, d]
                misc(mms, rd)

            def wo(u):
                b, i = divmod(u, 4)

                def mms():
                    pe.wait(loc["OT", u], tk["WA", L][6:10])
                    for c in range(4):
                        r = mm3(PS[:, 2, 0:D], [OTr[:, k, c] for k in range(2)], [WOF[:, c, k] for k in range(2)],
                                c == 0, c == 3, sig=c == 3)
                    loc[("OTfree",)] = [r]
                    return r

                def rd(m):
                    d = dve.do(lambda e: e.tensor_tensor(X[:, b, i], PS[:, 2, 0:D], X[:, b, i], ALU.add), m)
                    tk.setdefault(("FA", L, b), []).append(d)
                    return [d]
                misc(mms, rd)

            NU = 4 * NB
            for n in range(-1, NU + 2):
                A, B, C, Q = n, n - 1, n - 2, n + 1
                hA, hB, hC, hQ = 0 <= A < NU, 0 <= B < NU, 0 <= C < NU, 0 <= Q < NU
                if n == NU:
                    xt_free[0] = [loc["XTread", NB - 1], loc["XT", NB - 1, 0], loc["XT", NB - 1, 1]]
                    if NB > 1:
                        xt_free[0] += [loc["XTread", NB - 2], loc["XT", NB - 2, 0], loc["XT", NB - 2, 1]]
                    ahead()
                if hQ and Q % 4 in (1, 2) and Q // 4 + 1 < NB:
                    xt(Q // 4 + 1, Q % 4 - 1)
                if hA: scores(A, 0)
                if hC: pv(C, 3)
                if hQ: qk_post(Q, 0, 0, gemm(Q, 0, 0))
                if hB: ptrans(B, 0)
                if hA: scores(A, 1)
                if hQ: qk_post2(Q, 0)
                if hC: ot(C)
                if hB: pv(B, 0)
                if hQ: qk_post(Q, 1, 1, gemm(Q, 1, 1))
                if hQ: qk_post2(Q, 1)
                if hB: ptrans(B, 1)
                if hA: scores(A, 2)
                if hB: ptrans(B, 2)
                if hC: wo(C)
                if hA: scores(A, 3)
                if hB: pv(B, 1)
                if hQ: qkt(Q, 0)
                if hB: pv(B, 2)
                if hQ: qkt(Q, 1)
                if chores and hQ: chores.pop(0)()
                if hB: ptrans(B, 3)
                if hQ:
                    m = gemm(Q, 2, 0)
                    v = act.do(lambda e, Q=Q: e.copy(V[:, Q % 4], PS[:, 0, :]), m, lg(("Vfree", Q - 3)))
                    free[0] = [v]
                    loc["V", Q] = [v]
            barrier()

    def mlp_start(L):
        loc = {}
        w = xt_free[0]
        t_z = [dve.do(lambda e: e.memset(XS[0:1, :, 0, :], 0.0), w)]

        def lg(*names):
            return [loc[n] for n in names if n in loc]

        def shift(b):
            s = b % 2
            w = [get(("FA", L, b)), lg(("XSfree", b - 2)), xt_free[0]]
            loc["XS", b] = [ld.do(XS[1:P, s], X[0:P - 1, b, :, P:D], w), ld.do(XS[0:1, s, 1:4], X[P - 1:P, b, 0:3, P:D], w)]

        def stats(b):
            s = b % 2
            w = loc["XS", b] + t_z + xt_free[0]
            T = ST[:, s]
            ta = []
            for i in range(4):
                x = dve.do(lambda e, i=i: e.bn_stats(T[:, 12 * i:12 * i + 6], X[:, b, i, 0:P]), w, lg(("STfree", b - 2)))
                y = dve.do(lambda e, i=i: e.bn_stats(T[:, 12 * i + 6:12 * i + 12], XS[:, s, i]), w)
                ta.append((x, y))
            for i in range(4):
                z = dve.do(lambda e, i=i: e.bn_aggr(T[:, 64 + 2 * i:66 + 2 * i], T[:, 12 * i:12 * i + 12]), *ta[i])
            var = T[:, 64:72].rearrange("p (n s) -> p n s", s=2)[:, :, 1]
            r = T[:, 80:84]
            t1 = pool.do(lambda e: e.tensor_scalar(r, var, 1e-5, None, ALU.add), z)
            loc["rs", b] = [z, pool.do(lambda e: e.tensor_tensor(r, r, mhalf[:, 0:4], ALU.pow), t1)]

        def norm(b):
            s = b % 2
            T = ST[:, s]
            o = []
            for half, src in ((0, lambda i: X[:, b, i, 0:P]), (1, lambda i: XS[:, s, i])):
                for i in range(4):
                    o.append(dve.do(lambda e, i=i, half=half, src=src: e.tensor_scalar(
                        HN[:, s, i, half * P:(half + 1) * P], src(i), T[:, 64 + 2 * i:65 + 2 * i], T[:, 80 + i:81 + i],
                        ALU.subtract, ALU.mult), loc["rs", b], lg(("HNfree", b - 2)), xt_free[0]))
            loc["HN", b] = o
            loc["XSfree", b] = loc["STfree", b] = o

        shift(0)
        if NB > 1:
            shift(1)
        stats(0)
        norm(0)
        return loc, lg, shift, stats, norm

    def mlp(L, start, chores, ahead):
        with ExitStack() as c2:
            s2 = lambda n, s, d: c2.enter_context(nc.sbuf_tensor(f"{n}{L}", s, d))
            loc, lg, shift, stats, norm = start
            HT = s2("HT", [P, 2, 2, 2, S], F32R)
            TT = s2("TT", [P, S], F32)
            G = s2("G", [P, 2, S], F32)
            U = s2("U", [P, 2, S], F32)
            UR = s2("UR", [P, 2, 6, 2, S], F32R)
            Y = s2("Y", [P, 4, D], F32) if L == 1 else None
            LNT = s2("LNT", [P, 2, 64], F32)
            def ht(b, half, bank):
                s = b % 2
                pe.wait(free[bank], loc["HN", b])
                for i in range(4):
                    m = pe.do(lambda e, i=i: e.transpose(PS[:, bank, i * P:(i + 1) * P], HN[:, s, i, half * P:(half + 1) * P],
                                                         ident[:]), sig=i == 3)
                if half == 1:
                    loc["HNfree", b] = [m]
                d = dve.do(lambda e: e.tensor_scalar(TT[:], PS[:, bank, :], cols[:, L, 12 + half:13 + half],
                                                     cols[:, L, 14 + half:15 + half], ALU.mult, ALU.add), m, t_cols, lg(("TTfree",)))
                free[bank] = [d]
                w = lg(("W1done", b - 2))
                a = act.do(lambda e: e.copy(HT[:, s, half, 0], TT[:]), d, w)
                l = pool.do(lambda e: e.tensor_tensor(HT[:, s, half, 1], TT[:], f(HT[:, s, half, 0]), ALU.subtract), a, d, w)
                loc[("TTfree",)] = [a, l]
                loc["HT", b, half] = [a, l]

            def w1(b, c):
                s = b % 2
                banks = (2 * (c % 2), 2 * (c % 2) + 1)
                ms = []
                pe.wait(loc["HT", b, 0], loc["HT", b, 1], tk["WM", L])
                for bank, w in ((banks[1], 5 + c), (banks[0], c)) if c < 5 else ((banks[0], 10),):
                    pe.wait(free[bank])
                    for kc in range(2):
                        m = mm3(PS[:, bank, :], [W1[:, kc, k, w * P:(w + 1) * P] for k in range(2)],
                                [HT[:, s, kc, k] for k in range(2)], kc == 0, kc == 1, sig=kc == 1)
                    ms.append(m)
                if c == 5:
                    loc["W1done", b] = [m]
                q = c % 2
                n = P if c < 5 else 64
                gate = PS[:, banks[1], :] if c < 5 else PS[64:P, banks[0], :]
                bias = cols[:, L, 5 + c:6 + c] if c < 5 else cols[64:P, L, 10:11]
                a = act.do(lambda e: e.activation(G[0:n, q], gate, ACT.Gelu, bias=bias), ms[0], t_cols, lg(("Gfree", q)))
                d = dve.do(lambda e: e.scalar_tensor_tensor(
                    out=U[0:n, q], in0=PS[0:n, banks[0], :], scalar=cols[0:n, L, (c if c < 5 else 10):(c if c < 5 else 10) + 1],
                    in1=G[0:n, q], op0=ALU.add, op1=ALU.mult), ms[-1], a, lg(("Ufree", q)))
                if c < 5:
                    free[banks[1]] = [a]
                free[banks[0]] = [a, d]
                loc["Gfree", q] = [d]
                w = lg(("URfree", b - 2))
                h = act.do(lambda e: e.copy(UR[0:n, s, c, 0], U[0:n, q]), d, w)
                l = pool.do(lambda e: e.tensor_tensor(UR[0:n, s, c, 1], U[0:n, q], f(UR[0:n, s, c, 0]), ALU.subtract), h, d, w)
                loc["Ufree", q] = [h, l]
                loc.setdefault(("U", b), []).extend([h, l])

            def w2(b, i):
                s = b % 2
                bank = 4 + i % 2
                pe.wait(free[bank], loc["U", b])
                for c in range(6):
                    n = P if c < 5 else 64
                    m = mm3(PS[:, bank, 0:D], [UR[0:n, s, c, k, i * P:(i + 1) * P] for k in range(2)],
                            [W2[0:n, c, k] for k in range(2)], c == 0, c == 5, sig=c == 5)
                if i == 3:
                    loc["URfree", b] = [m]
                d = dve.do(lambda e: e.tensor_tensor(X[:, b, i], PS[:, bank, 0:D], X[:, b, i], ALU.add), m, loc["XB", b])
                free[bank] = [d]
                loc["Xd", b, i] = d
                tk.setdefault(("FX", L + 1, b), []).append(d)
                if L == 1 and i % 2:
                    tiles = [X[:, b, j] for j in (i - 1, i)]
                    l = layernorm(tiles, tiles, LNT[:, i // 2], [loc["Xd", b, i - 1], d, get(("LNread", i // 2))])()
                    tk[("LNread", i // 2)] = [l]
                    st.do(t["out"][b, (i - 1) * P:(i + 1) * P].rearrange("(t p) d -> p t d", p=P), X[:, b, i - 1:i + 1], l)

            def residual(b):
                w = [loc["HN", b], loc["XS", b]]
                r = [pool.do(lambda e, i=i: e.tensor_tensor(X[:, b, i], X[:, b, i], b2[:, L], ALU.add), w, t_cols) for i in range(4)]
                if L == 1:
                    y = ld.do(Y[:], t["x2s"][b], lg(("Yfree",)))
                    r = [pool.do(lambda e, i=i: e.tensor_tensor(X[:, b, i], X[:, b, i], Y[:, i], ALU.add), y, r[i]) for i in range(4)]
                    loc[("Yfree",)] = r
                loc["XB", b] = r

            ht(0, 0, 6)
            ht(0, 1, 7)
            for b in range(NB + 1):
                if b == NB:
                    xt_free[0] = [loc["HN", b] for b in range(NB)] + [loc["HNfree", b] for b in range(NB)]
                    ahead()
                for c in range(6):
                    if b < NB:
                        w1(b, c)
                    if b < NB and c == 3:
                        residual(b)
                    if b + 1 < NB and c == 0:
                        stats(b + 1)
                    if b + 1 < NB and c == 1:
                        norm(b + 1)
                        if b + 2 < NB:
                            shift(b + 2)
                    if b + 1 < NB and c in (2, 3):
                        ht(b + 1, c - 2, 4 + c)
                    if b >= 1 and c in (1, 2, 3, 4):
                        w2(b - 1, c - 1)
                    if chores and c % 2 and b >= 1:
                        chores.pop(0)()
            assert not chores
            barrier()

    chores = load_attn(0, [], dve)
    starts = [attention_start(0)]
    for c in chores[:6]:
        c()
    chores = [chores[6:8], chores[8:10]] + load_mlp(0, [], pool)
    chores[:2] = [lambda p=p: [c() for c in p] for p in chores[:2]]
    for L in range(2):
        attention(L, starts.pop(), chores, lambda: starts.append(mlp_start(L)))
        while chores:
            chores.pop(0)()
        if stop == f"fa{L}":
            for b in range(NB):
                st.do(t["out"][b].rearrange("(t p) d -> p t d", p=P), X[:, b], tk["FA", L, b])
            return
        start = starts.pop()
        if L == 0:
            tk["rot", 1] = rotations(1, [])
            mlp(0, start, load_attn(1, [], pool), lambda: starts.append(attention_start(1)))
        else:
            mlp(1, start, [], lambda: None)
        if stop == f"fm{L}":
            for b in range(NB):
                st.do(t["out"][b].rearrange("(t p) d -> p t d", p=P), X[:, b], tk["FX", L + 1, b])
            return
        if L == 0:
            chores = load_mlp(1, [], pool)


def queues_end(nc, ctx, pe, act, dve, pool, sp, ld, st):
    sp.wait(*st.all(), *ld.all())
    block = ctx.enter_context(nc.Block())
    block.tensor(pe.play)
    block.scalar(act.play)
    block.vector(dve.play)
    block.gpsimd(pool.play)
    block.sync(sp.play)


def constants():
    n = np.arange(S, dtype=np.float32)
    inv = (1.0 / np.power(np.float32(10000.0), np.arange(0, 16, 2, dtype=np.float32) / np.float32(16))).astype(np.float32)
    fr = n[:, None] * inv[None, :]
    sin, cos = np.sin(fr), np.cos(fr)
    tab = np.zeros((P, 2, S), np.float32)
    for r in range(P):
        tab[r, 0], tab[r, 1] = cos[:, r % 16 // 2], sin[:, r % 16 // 2]
    hi = np.arange(0, 64, 2, dtype=np.float32)
    inv = (np.float32(1.0) / np.power(np.float32(10000.0), hi / np.float32(64))).astype(np.float32)
    fr = n[:, None] * inv[None, :]
    base = (hi + np.float32(0.4 * 64)) / np.float32(1.4 * 64)
    scale = np.power(base[None, :], ((n - 256) / np.float32(64))[:, None]).astype(np.float32)
    cos, sin = np.cos(fr), np.sin(fr)
    rot = np.stack([np.concatenate(v, 1) for v in (
        (cos * scale * 8, cos * scale * 8), (-sin * scale * 8, sin * scale * 8),
        (cos / scale, cos / scale), (-sin / scale, sin / scale))]).astype(np.float32)
    rot = np.ascontiguousarray(rot.reshape(4, 4, P, 64).transpose(2, 0, 1, 3))
    q, k = np.arange(P)[:, None], np.arange(256)[None, :]
    mask = np.where((k < P) & (k < q) | (k >= P) & (k - P > q), np.float32(NEG), np.float32(0)).astype(np.float32)
    return {"c_rot": rot, "c_mask": mask, "c_ident": np.eye(P, dtype=np.float32), "c_tab": tab}


def layout(inputs, NB=8):
    c = np.ascontiguousarray
    i = {k: np.asarray(v) for k, v in inputs.items()}
    a = constants()
    a["x"] = c(i["x"][:NB])
    a["ctxT"] = c(i["ctx_1024"][:NB].reshape(NB * S, D).T)
    for j, n in enumerate("qkv"):
        a["s_" + n] = c(i["L0_attn_w_qkv"][:, j * D:(j + 1) * D])
    a["s_o"] = c(i["L0_attn_w_proj"])
    for n in "qkvo":
        a["x_" + n] = c(i["L0_xattn_W" + n].T)
    a["xbqk"] = c(np.concatenate([i["L0_xattn_bq"].reshape(2, P), i["L0_xattn_bk"].reshape(2, P)]).T)
    a["xbvo"] = c(np.stack([np.broadcast_to(i["L0_xattn_b" + n], (P, D)) for n in "vo"], 1))
    qs, ks = i["L0_ffn_q_scale"], i["L0_ffn_k_scale"]
    sw = lambda v: np.concatenate([v[:, 32:], v[:, :32]], 1)
    qk = np.stack([qs, sw(qs), ks, sw(ks)], 1)
    a["f_qks"] = c(np.broadcast_to(qk[None], (P, 2, 4, 64)))
    a["f_wqkv"] = c(i["L0_ffn_wqkv"])
    a["f_wo"] = c(i["L0_ffn_wo"])
    H = i["L0_ffn_w2"].shape[1]
    def hidden(w):
        w = w.reshape(w.shape[:-1] + (2, H))
        o = np.zeros(w.shape[:-2] + (11 * P,), np.float32)
        o[..., :640], o[..., 640:1280] = w[..., 0, :640], w[..., 1, :640]
        o[..., 1280:1280 + H - 640], o[..., 1344:1344 + H - 640] = w[..., 0, 640:], w[..., 1, 640:]
        return o

    a["f_w1"] = hidden(i["L0_ffn_w1"])
    w2 = np.zeros((2, 768, D), np.float32)
    w2[:, :H] = i["L0_ffn_w2"]
    cols = np.concatenate([hidden(i["L0_ffn_b1"]).reshape(2, 11, P), np.zeros((2, 1, P), np.float32), i["L0_ffn_ln_g"].reshape(2, 2, P), i["L0_ffn_ln_b"].reshape(2, 2, P)], 1)
    a["f_w2"] = w2
    a["f_cols"] = c(cols.transpose(2, 0, 1))
    a["f_b2"] = c(np.broadcast_to(i["L0_ffn_b2"][None], (P, 2, D)))
    return a


def kernel(**inputs):
    import concourse.bacc as bacc
    from concourse.bass_utils import run_bass_kernel_spmd

    arrays = layout(inputs)
    nc = bacc.Bacc("TRN2", target_bir_lowering=False, num_devices=1)
    t = {k: nc.dram_tensor(k, a.shape, mybir.dt.from_np(a.dtype), kind="ExternalInput").ap() for k, a in arrays.items()}
    t["out"] = nc.dram_tensor("out", (8, S, D), F32, kind="ExternalOutput").ap()
    t["x2s"] = nc.dram_tensor("x2s", (8, P, 4, D), F32, kind="Internal").ap()
    t["hs"] = nc.dram_tensor("hs", (2, 4, P, 3, S), BF16, kind="Internal").ap()
    build(nc, t, 8)
    r = run_bass_kernel_spmd(nc, [arrays], core_ids=[0])
    return r.results[0]["out"]
```
